# Optimizing a Trainium2 kernel written in Bass

```python
import numpy as np
import jax
import jax.numpy as jnp

def _softmax(x, axis=-1):
    return jax.nn.softmax(x, axis=axis)

def _gelu(x):
    return jax.nn.gelu(x, approximate=True)

def _silu(x):
    return jax.nn.silu(x)

def _sigmoid(x):
    return jax.nn.sigmoid(x)

def _layernorm(x, axis=-1, eps=1e-05):
    m = jnp.mean(x, axis=axis, keepdims=True)
    v = jnp.var(x, axis=axis, keepdims=True)
    return (x - m) / jnp.sqrt(v + eps)

def _scatter_add(tgt, idx, src, axis=0):
    return tgt.at[idx].add(src)

def _segment_sum(src, seg, n):
    return jax.ops.segment_sum(src, seg, n)
kernel_name = 'mk_cond_resid_d4_seqx_r4_9261a8'

def setup_inputs(seed: int=0):
    np.random.seed(seed)
    _w = jnp.asarray

    def _rec_inputs():
        import jax
        import jax.numpy as jnp
        _rk = jax.random.key(seed)
        x = 4.136e-05 + 0.9999 * jax.random.normal(jax.random.fold_in(_rk, 1), (8, 256, 256), jnp.float32)
        _lenS = 256 - jax.random.randint(jax.random.fold_in(_rk, 7), (8,), 0, max(1, 256 // 4) + 1, jnp.int32)
        _lenS2 = 256 - jax.random.randint(jax.random.fold_in(_rk, 8), (8,), 0, max(1, 256 // 4) + 1, jnp.int32)
        cond_1024 = -0.00608245 + 1.00131 * jax.random.normal(jax.random.fold_in(_rk, 11), (8, 256), jnp.float32)
        return (x, cond_1024)
    x, cond_1024 = _rec_inputs()

    def _L0_cond_setup():
        import jax, jax.numpy as jnp
        import numpy as np
        B, T, D_IN, V_IN, E = (64, 128, 256, 256, 256)
        key = jax.random.key(seed)
        ks = jax.random.split(key, 16)
        s = 0.01
        return {'video': jax.random.normal(ks[0], (B, V_IN), jnp.float32), 'seq': jax.random.normal(ks[1], (B, T, D_IN), jnp.float32), 'W_z': jax.random.normal(ks[2], (D_IN, E), jnp.float32) * s, 'U_z': jax.random.normal(ks[3], (E, E), jnp.float32) * s, 'C_z': jax.random.normal(ks[4], (V_IN, E), jnp.float32) * s, 'b_z': jnp.zeros((E,), jnp.float32), 'W_r': jax.random.normal(ks[5], (D_IN, E), jnp.float32) * s, 'U_r': jax.random.normal(ks[6], (E, E), jnp.float32) * s, 'C_r': jax.random.normal(ks[7], (V_IN, E), jnp.float32) * s, 'b_r': jnp.zeros((E,), jnp.float32), 'W': jax.random.normal(ks[8], (D_IN, E), jnp.float32) * s, 'U': jax.random.normal(ks[9], (E, E), jnp.float32) * s, 'C': jax.random.normal(ks[10], (V_IN, E), jnp.float32) * s, 'b': jnp.zeros((E,), jnp.float32)}
    _L0_cond_all = _L0_cond_setup()
    _L0_cond_in = {k: v for k, v in _L0_cond_all.items() if k in ('W_z', 'U_z', 'C_z', 'b_z', 'W_r', 'U_r', 'C_r', 'b_r', 'W', 'U', 'C', 'b')}
    del _L0_cond_all

    def _L1_cond_setup():
        import jax, jax.numpy as jnp
        import numpy as np
        EPS = 1e-08
        key = jax.random.key(seed)
        ks = jax.random.split(key, 8)
        B, S, D, H = (8, 512, 256, 256)
        scale = 1.0 / np.sqrt(D)
        return {'input_seq': jax.random.normal(ks[0], (B, S, D), dtype=jnp.float32), 'initial_hidden': jax.random.normal(ks[1], (B, H), dtype=jnp.float32), 'W_f': jax.random.normal(ks[2], (H, D), dtype=jnp.float32) * scale, 'b_f': jnp.zeros((H,), dtype=jnp.float32), 'W_i': jax.random.normal(ks[3], (H, D), dtype=jnp.float32) * scale, 'b_i': jnp.zeros((H,), dtype=jnp.float32), 'W_h': jax.random.normal(ks[4], (H, D), dtype=jnp.float32) * scale, 'b_h': jnp.zeros((H,), dtype=jnp.float32)}
    _L1_cond_all = _L1_cond_setup()
    _L1_cond_in = {k: v for k, v in _L1_cond_all.items() if k in ('W_f', 'b_f', 'W_i', 'b_i', 'W_h', 'b_h')}
    del _L1_cond_all

    def _L2_cond_setup():
        import jax, jax.numpy as jnp
        import numpy as np
        B, L, D_IN, D = (64, 128, 256, 256)
        key = jax.random.key(seed)
        k1, k2, k3, k4, k5 = jax.random.split(key, 5)
        x = jax.random.normal(k1, (B, L, D_IN), dtype=jnp.float32)
        Wk = jax.random.normal(k2, (D_IN, 3 * D), dtype=jnp.float32) * (1.0 / np.sqrt(D_IN))
        Wr = jax.random.normal(k3, (D, 3 * D), dtype=jnp.float32) * (1.0 / np.sqrt(D))
        c0 = jax.random.normal(k4, (B, D), dtype=jnp.float32)
        h0 = jax.random.normal(k5, (B, D), dtype=jnp.float32)
        return {'x': x, 'Wk': Wk, 'Wr': Wr, 'c0': c0, 'h0': h0}
    _L2_cond_all = _L2_cond_setup()
    _L2_cond_in = {k: v for k, v in _L2_cond_all.items() if k in ('Wk', 'Wr')}
    del _L2_cond_all

    def _L3_cond_setup():
        import jax, jax.numpy as jnp
        import numpy as np
        NUM_EXPERTS = 4
        TOP_K = 2
        key = jax.random.key(seed)
        ks = jax.random.split(key, 16)
        B, L, D, E, H = (8, 192, 256, NUM_EXPERTS, 1024)
        s = 0.02
        return {'context_c': jax.random.normal(ks[0], (B, L, D), jnp.float32), 'time_cond': jax.random.normal(ks[1], (B, D), jnp.float32), 'gate_w': jax.random.normal(ks[2], (3 * D, E), jnp.float32) * s, 'gate_b': jnp.zeros((E,), jnp.float32), 'time_w': jax.random.normal(ks[3], (D, 2 * E), jnp.float32) * s, 'time_b': jnp.zeros((2 * E,), jnp.float32), 'ew1': jax.random.normal(ks[4], (E, D, H), jnp.float32) * s, 'eb1': jnp.zeros((E, H), jnp.float32), 'ew2': jax.random.normal(ks[5], (E, H, D), jnp.float32) * s, 'eb2': jnp.zeros((E, D), jnp.float32), 'sw1': jax.random.normal(ks[6], (D, H), jnp.float32) * s, 'sb1': jnp.zeros((H,), jnp.float32), 'sw2': jax.random.normal(ks[7], (H, D), jnp.float32) * s, 'sb2': jnp.zeros((D,), jnp.float32)}
    _L3_cond_all = _L3_cond_setup()
    _L3_cond_in = {k: v for k, v in _L3_cond_all.items() if k in ('gate_w', 'gate_b', 'time_w', 'time_b', 'ew1', 'eb1', 'ew2', 'eb2', 'sw1', 'sb1', 'sw2', 'sb2')}
    del _L3_cond_all
    return {'x': x, 'cond_1024': cond_1024, 'L0_cond_W_z': _L0_cond_in['W_z'], 'L0_cond_U_z': _L0_cond_in['U_z'], 'L0_cond_C_z': _L0_cond_in['C_z'], 'L0_cond_b_z': _L0_cond_in['b_z'], 'L0_cond_W_r': _L0_cond_in['W_r'], 'L0_cond_U_r': _L0_cond_in['U_r'], 'L0_cond_C_r': _L0_cond_in['C_r'], 'L0_cond_b_r': _L0_cond_in['b_r'], 'L0_cond_W': _L0_cond_in['W'], 'L0_cond_U': _L0_cond_in['U'], 'L0_cond_C': _L0_cond_in['C'], 'L0_cond_b': _L0_cond_in['b'], 'L1_cond_W_f': _L1_cond_in['W_f'], 'L1_cond_b_f': _L1_cond_in['b_f'], 'L1_cond_W_i': _L1_cond_in['W_i'], 'L1_cond_b_i': _L1_cond_in['b_i'], 'L1_cond_W_h': _L1_cond_in['W_h'], 'L1_cond_b_h': _L1_cond_in['b_h'], 'L2_cond_Wk': _L2_cond_in['Wk'], 'L2_cond_Wr': _L2_cond_in['Wr'], 'L3_cond_gate_w': _L3_cond_in['gate_w'], 'L3_cond_gate_b': _L3_cond_in['gate_b'], 'L3_cond_time_w': _L3_cond_in['time_w'], 'L3_cond_time_b': _L3_cond_in['time_b'], 'L3_cond_ew1': _L3_cond_in['ew1'], 'L3_cond_eb1': _L3_cond_in['eb1'], 'L3_cond_ew2': _L3_cond_in['ew2'], 'L3_cond_eb2': _L3_cond_in['eb2'], 'L3_cond_sw1': _L3_cond_in['sw1'], 'L3_cond_sb1': _L3_cond_in['sb1'], 'L3_cond_sw2': _L3_cond_in['sw2'], 'L3_cond_sb2': _L3_cond_in['sb2']}

def reference(x, cond_1024, L0_cond_W_z, L0_cond_U_z, L0_cond_C_z, L0_cond_b_z, L0_cond_W_r, L0_cond_U_r, L0_cond_C_r, L0_cond_b_r, L0_cond_W, L0_cond_U, L0_cond_C, L0_cond_b, L1_cond_W_f, L1_cond_b_f, L1_cond_W_i, L1_cond_b_i, L1_cond_W_h, L1_cond_b_h, L2_cond_Wk, L2_cond_Wr, L3_cond_gate_w, L3_cond_gate_b, L3_cond_time_w, L3_cond_time_b, L3_cond_ew1, L3_cond_eb1, L3_cond_ew2, L3_cond_eb2, L3_cond_sw1, L3_cond_sb1, L3_cond_sw2, L3_cond_sb2):
    import jax
    import jax.numpy as jnp

    def _L0_cond_ref(video, seq, W_z, U_z, C_z, b_z, W_r, U_r, C_r, b_r, W, U, C, b):
        import jax, jax.numpy as jnp
        import numpy as np
        B, T, D_IN, V_IN, E = (64, 128, 256, 256, 256)
        vz = video @ C_z + b_z
        vr = video @ C_r + b_r
        vh = video @ C + b
        xz = jnp.einsum('btd,de->bte', seq, W_z)
        xr = jnp.einsum('btd,de->bte', seq, W_r)
        xh = jnp.einsum('btd,de->bte', seq, W)

        def step(h, xs):
            xzt, xrt, xht = xs
            z = jax.nn.sigmoid(xzt + h @ U_z + vz)
            r = jax.nn.sigmoid(xrt + h @ U_r + vr)
            hh = jnp.tanh(xht + r * h @ U + vh)
            h_new = (1.0 - z) * h + z * hh
            return (h_new, h_new)
        h0 = jnp.zeros((seq.shape[0], U.shape[0]), seq.dtype)
        xs = (jnp.swapaxes(xz, 0, 1), jnp.swapaxes(xr, 0, 1), jnp.swapaxes(xh, 0, 1))
        _, out_t = jax.lax.scan(step, h0, xs)
        return jnp.swapaxes(out_t, 0, 1)

    def _L1_cond_ref(input_seq, initial_hidden, W_f, b_f, W_i, b_i, W_h, b_h):
        import jax, jax.numpy as jnp
        import numpy as np
        EPS = 1e-08
        forget_gate = jax.nn.sigmoid(jnp.einsum('bsd,hd->bsh', input_seq, W_f) + b_f)
        input_gate = jax.nn.sigmoid(jnp.einsum('bsd,hd->bsh', input_seq, W_i) + b_i)
        gate_sum = forget_gate + input_gate + EPS
        forget_norm = forget_gate / gate_sum
        input_norm = input_gate / gate_sum
        candidate = jnp.einsum('bsd,hd->bsh', input_seq, W_h) + b_h
        new_info = input_norm * candidate
        log_ret = jnp.log(forget_norm + EPS)
        log_cumprod = jnp.cumsum(log_ret, axis=1)
        B, _, H = log_cumprod.shape
        padded = jnp.concatenate([jnp.zeros((B, 1, H), dtype=log_cumprod.dtype), log_cumprod], axis=1)
        scaling = jnp.exp(log_cumprod[:, -1:, :] - padded[:, :-1, :])
        hidden = jnp.cumsum(scaling * new_info, axis=1)
        hidden = hidden + jnp.exp(log_cumprod) * initial_hidden[:, None, :]
        return hidden

    def _L2_cond_ref(x, Wk, Wr, c0, h0):
        import jax, jax.numpy as jnp
        import numpy as np
        B, L, D_IN, D = (64, 128, 256, 256)
        x_proj = jnp.einsum('bli,ig->blg', x, Wk)

        def step(carry, xp_t):
            c, h = carry
            gates = xp_t + h @ Wr
            f, o, g = jnp.split(gates, 3, axis=-1)
            sf = jax.nn.sigmoid(f)
            c_new = c * sf + (1.0 - sf) * jnp.tanh(g)
            h_new = jax.nn.sigmoid(o) * jnp.tanh(c_new)
            return ((c_new, h_new), h_new)
        _, hs = jax.lax.scan(step, (c0, h0), jnp.swapaxes(x_proj, 0, 1))
        return jnp.swapaxes(hs, 0, 1)

    def _L3_cond_ref(context_c, time_cond, gate_w, gate_b, time_w, time_b, ew1, eb1, ew2, eb2, sw1, sb1, sw2, sb2):
        import jax, jax.numpy as jnp
        import numpy as np
        NUM_EXPERTS = 4
        TOP_K = 2
        B, L, D = context_c.shape
        E, K = (NUM_EXPERTS, TOP_K)
        L_head = L_wrist = L // 3
        head = context_c[:, :L_head]
        wrist = context_c[:, L_head:L_head + L_wrist]
        proprio = context_c[:, L_head + L_wrist:]
        full_agg = context_c.mean(axis=1)
        hp_agg = jnp.concatenate([head, proprio], axis=1).mean(axis=1)
        wp_agg = jnp.concatenate([wrist, proprio], axis=1).mean(axis=1)
        gate_in = jnp.concatenate([full_agg, hp_agg, wp_agg], axis=-1)
        gate_logits = gate_in @ gate_w + gate_b
        mod = jax.nn.silu(time_cond) @ time_w + time_b
        scale, shift = jnp.split(mod, 2, axis=-1)
        gate_logits = gate_logits * (1.0 + scale) + shift
        gate_scores = jax.nn.softmax(gate_logits, axis=-1)
        topk_w, topk_i = jax.lax.top_k(gate_scores, K)
        topk_w = topk_w / (topk_w.sum(axis=-1, keepdims=True) + 1e-08)
        onehot = (topk_i[..., None] == jnp.arange(E)[None, None, :]).astype(context_c.dtype)
        w_be = jnp.sum(topk_w[..., None] * onehot, axis=1)
        mask = np.ones((E, L), dtype=np.float32)
        mask[1, L_head:L_head + L_wrist] = 0.0
        mask[2, :L_head] = 0.0
        mask = jnp.asarray(mask)
        out = jnp.zeros_like(context_c)
        for e in range(E):
            h = jax.nn.gelu(context_c @ ew1[e] + eb1[e], approximate=True)
            y = h @ ew2[e] + eb2[e]
            out = out + w_be[:, e][:, None, None] * mask[e][None, :, None] * y
        shared = jax.nn.gelu(context_c @ sw1 + sb1, approximate=True) @ sw2 + sb2
        return out + shared
    x = x + _L0_cond_ref(cond_1024, x, L0_cond_W_z, L0_cond_U_z, L0_cond_C_z, L0_cond_b_z, L0_cond_W_r, L0_cond_U_r, L0_cond_C_r, L0_cond_b_r, L0_cond_W, L0_cond_U, L0_cond_C, L0_cond_b)
    x = x + _L1_cond_ref(x, cond_1024, L1_cond_W_f, L1_cond_b_f, L1_cond_W_i, L1_cond_b_i, L1_cond_W_h, L1_cond_b_h)
    x = x + _L2_cond_ref(x, L2_cond_Wk, L2_cond_Wr, cond_1024, cond_1024)
    x = x + _L3_cond_ref(x, cond_1024, L3_cond_gate_w, L3_cond_gate_b, L3_cond_time_w, L3_cond_time_b, L3_cond_ew1, L3_cond_eb1, L3_cond_ew2, L3_cond_eb2, L3_cond_sw1, L3_cond_sb1, L3_cond_sw2, L3_cond_sb2)
    return x

_drawn_inputs = setup_inputs


def setup_inputs(seed=0):
    import zlib

    import numpy as np

    out = dict(_drawn_inputs(seed))
    spreads = {'L0_cond_b_z': (0.0, 2.0),
     'L0_cond_b_r': (0.0, 2.0),
     'L0_cond_b': (0.0, 0.1),
     'L1_cond_b_f': (0.0, 2.0),
     'L1_cond_b_i': (0.0, 2.0),
     'L1_cond_b_h': (0.0, 2.0),
     'L3_cond_gate_b': (0.0, 0.1),
     'L3_cond_time_b': (0.0, 0.1),
     'L3_cond_eb1': (0.0, 0.372),
     'L3_cond_eb2': (0.0, 0.1),
     'L3_cond_sb1': (0.0, 0.1),
     'L3_cond_sb2': (0.0, 0.1)}
    factors = {'L0_cond_W_z': 7.08,
     'L0_cond_U_z': 44.523,
     'L0_cond_C_z': 8.0,
     'L0_cond_W_r': 24.781,
     'L0_cond_U_r': 64.0,
     'L0_cond_C_r': 29.16,
     'L0_cond_U': 4.033,
     'L1_cond_W_f': 5.573,
     'L1_cond_W_i': 5.311,
     'L1_cond_W_h': 2.859}
    for name, (base, spread) in spreads.items():
        noise = np.random.default_rng([zlib.crc32(name.encode()), seed]).standard_normal(out[name].shape)
        drawn = base * np.exp(spread * noise) if base else spread * noise
        out[name] = jnp.asarray(drawn.astype(out[name].dtype))
    for name, factor in factors.items():
        out[name] = (out[name] * factor).astype(out[name].dtype)
    return out
```

```python
from contextlib import ExitStack

import concourse.bass as bass
from concourse import mybir

F32 = mybir.dt.float32
F16 = mybir.dt.float16
ACT = mybir.ActivationFunctionType
ALU = mybir.AluOpType
AX_X = mybir.AxisListType.X

P = 128
B, T, D = 8, 256, 256
K = D // P
TOK = B * T
SPLIT_SCALE = 64.0
UNSCALE = 1.0 / SPLIT_SCALE
EPS = 1e-8
E = 4
HID = 1024
FC = HID // P
NT = 512
TT = NT // B
N_TILES = TOK // NT
SUB = NT // P
UNROLL = 4
L_HEAD = T // 3
L_PROPRIO = T - 2 * L_HEAD
STAGE = 1024
N_STAGE = 2
WK_PIECE = 2 * -(-K * 3 * D // STAGE)
N_BLOCKS = (E + 1) * FC


def build(nc, xT, condT, w0, u0, c0, b0, w1, b1, wk, wr, gate_w, time_w, small_b, eb1, eb2,
          ew1, ew2, ident, bsel, lower, mask_tok, mask_col, out):
    with ExitStack() as ctx:
        def sb(name, shape, dt=F32):
            return ctx.enter_context(nc.sbuf_tensor(name, shape, dt))

        def sem(name):
            return ctx.enter_context(nc.semaphore(name))

        X = sb("X", [P, K, TOK])
        XS = sb("XS", [P, 2 * K * TOK], F16)
        Xh = XS[:, 0:K * TOK].rearrange("p (k n) -> p k n", k=K)
        Xl = XS[:, K * TOK:2 * K * TOK].rearrange("p (k n) -> p k n", k=K)
        bufD = XS[:, :].bitcast(F32).rearrange("p (k n) -> p k n", k=K)
        pre = sb("pre", [P, 3 * K * TOK])
        pre16 = pre[:, :].bitcast(F16)
        PREh = pre16[:, 0:T * 48].rearrange("p (t c) -> p t c", c=48)
        PREl = pre16[:, T * 48:2 * T * 48].rearrange("p (t c) -> p t c", c=48)
        bufA, bufB, bufC = (pre[:, i * K * TOK:(i + 1) * K * TOK].rearrange("p (k n) -> p k n", k=K)
                            for i in range(3))
        preproj = sb("preproj", [P, NT])
        G = pre[:, 0:2 * NT].rearrange("p (s n) -> p s n", s=2)
        Gh = pre16[:, 4 * NT:6 * NT].rearrange("p (s n) -> p s n", s=2)
        Gl = pre16[:, 6 * NT:8 * NT].rearrange("p (s n) -> p s n", s=2)
        ACC = pre[:, 4 * NT:4 * NT + SUB * D].rearrange("p (s n) -> p s n", s=SUB)
        stage = sb("stage", [P, N_STAGE, STAGE])
        W0h, W0l = sb("W0h", [P, K, 3 * D], F16), sb("W0l", [P, K, 3 * D], F16)
        U0h, U0l = sb("U0h", [P, K, 3 * D], F16), sb("U0l", [P, K, 3 * D], F16)
        W1h, W1l = sb("W1h", [P, K, 3 * D], F16), sb("W1l", [P, K, 3 * D], F16)
        Wkh, Wkl = W0h, W0l
        Wrh, Wrl = sb("Wrh", [P, K, 3 * D], F16), sb("Wrl", [P, K, 3 * D], F16)
        E1h, E1l = sb("E1h", [P, E + 1, K * HID], F16), sb("E1l", [P, E + 1, K * HID], F16)
        E2h, E2l = sb("E2h", [P, E + 1, FC * D], F16), sb("E2l", [P, E + 1, FC * D], F16)
        I = sb("I", [P, P], F32)
        I64 = sb("I64", [P, P], F16)
        cond = sb("cond", [P, K, B])
        v0 = sb("v0", [P, 3 * K, B])
        b0s = sb("b0s", [P, 3 * K])
        b1s = sb("b1s", [P, 3 * K])
        eb1s = sb("eb1s", [P, (E + 1) * FC])
        hh_ = sb("h_hi", [P, K * B], F16)
        hl_ = sb("h_lo", [P, K * B], F16)
        h32 = sb("h32", [P, K * B])
        rhh, rhl, rh32 = sb("rh_hi", [P, K * B], F16), sb("rh_lo", [P, K * B], F16), sb("rh32", [P, K * B])
        gr, gz, gh = sb("gr", [P, K * B]), sb("gz", [P, K * B]), sb("gh", [P, K * B])
        nah, zh = sb("nah", [P, K * B]), sb("zh", [P, K * B])
        zeros, eps, mark = sb("zeros", [P, T]), sb("eps", [P, 1]), sb("mark", [P, 8])
        cell, tcell = sb("cell", [P, K * B]), sb("tcell", [P, K * B])
        sgc, silu = sb("sgc", [P, K, B]), sb("silu", [P, K, B])
        gws = sb("gws", [P, 3 * K, E])
        tws = sb("tws", [P, K, 2 * E])
        sbb = sb("sbb", [B, 3 * E])
        seg = sb("seg", [P, 3, K * B])
        agg = sb("agg", [P, 3, K * B])
        lg, mod, ex, sc = sb("lg", [B, E]), sb("mod", [B, 2 * E]), sb("ex", [B, E]), sb("sc", [B, E])
        mx, sm, rs = sb("mx", [B, 1]), sb("sm", [B, 1]), sb("rs", [B, 1])
        g3, q3, low = sb("g3", [B, E, E]), sb("q3", [B, E, E]), sb("low", [B, E * E])
        rank, sel5 = sb("rank", [B, E]), sb("sel5", [B, E + 1])
        bs = sb("bs", [B, P])
        mtok, wtok = sb("mtok", [P, T * B // P, E]), sb("wtok", [P, T * B // P, E])
        mcol = sb("mcol", [E + 1, TOK], F16)
        wc = sb("wc", [E + 1, P])
        wch, wcl = sb("wch", [E + 1, P], F16), sb("wcl", [E + 1, P], F16)
        wcolh, wcoll = (pre16[0:E + 1, (4 + i) * TOK:(5 + i) * TOK] for i in range(2))
        eb2s, eb2h, eb2l = sb("eb2s", [E + 1, D]), sb("eb2h", [E + 1, D], F16), sb("eb2l", [E + 1, D], F16)
        bank = [ctx.enter_context(nc.psum_tensor(f"bank{i}", [P, 512], F32)) for i in range(8)]

        in_w0, in_u0, in_small, in_late = sem("in_w0"), sem("in_u0"), sem("in_small"), sem("in_late")
        in_x = [sem(f"in_x{i}") for i in range(N_TILES)]
        staged = [sem(f"staged{i}") for i in range(N_STAGE)]
        stage_free = sem("stage_free")
        late_split = sem("late_split")
        out_done = sem("out_done")
        dve_step, pool_step, act_step = sem("dve_step"), sem("pool_step"), sem("act_step")
        w0_ready, u0_ready, x0_split = sem("w0_ready"), sem("u0_ready"), sem("x0_split")
        v_psum, v_ready, p0_psum, p0_free = (sem(n) for n in (
            "v_psum", "v_ready", "p0_psum", "p0_free"))
        r_psum, z_psum, hh_psum = sem("r_psum"), sem("z_psum"), sem("hh_psum")
        r_sig, z_sig, hh_tanh = sem("r_sig"), sem("z_sig"), sem("hh_tanh")
        rh_hi_ready, rh_32_ready, rh_lo_ready = sem("rh_hi_ready"), sem("rh_32_ready"), sem("rh_lo_ready")
        nah_ready, zh_ready = sem("nah_ready"), sem("zh_ready")
        h_hi_ready, h_32_ready, h_lo_ready = sem("h_hi_ready"), sem("h_32_ready"), sem("h_lo_ready")
        x1_added = sem("x1_added")
        x1_split, p1_psum, p1_free = sem("x1_split"), sem("p1_psum"), sem("p1_free")
        gates1, logs1, lc1, exps1, elc1 = (sem(n) for n in ("gates1", "logs1", "lc1", "exps1", "elc1"))
        norm1 = sem("norm1")
        x2_split, p2_psum, p2_hi, p2_free = sem("x2_split"), sem("p2_psum"), sem("p2_hi"), sem("p2_free")
        g_psum, f_psum, o_psum = sem("g_psum"), sem("f_psum"), sem("o_psum")
        g_tanh, f_sig, o_sig, c_tanh = sem("g_tanh"), sem("f_sig"), sem("o_sig"), sem("c_tanh")
        d_ready, m_ready, c_ready = sem("d_ready"), sem("m_ready"), sem("c_ready")
        s_hi_ready, s_32_ready, s_lo_ready = sem("s_hi_ready"), sem("s_32_ready"), sem("s_lo_ready")
        x3_added = sem("x3_added")
        x3_split, silu_ready, agg_ready, gate_psum = (sem(n) for n in (
            "x3_split", "silu_ready", "agg_ready", "gate_psum"))
        sgc_ready, mx_ready, ex_ready, sel_ready, wsel_psum, w_ready = (sem(n) for n in (
            "sgc_ready", "mx_ready", "ex_ready", "sel_ready", "wsel_psum", "w_ready"))
        up_psum, gelu_ready, gh_ready, gl_ready, down_done, y_psum, y_free, out_ready = (sem(n) for n in (
            "up_psum", "gelu_ready", "gh_ready", "gl_ready", "down_done", "y_psum", "y_free", "out_ready"))

        block = ctx.enter_context(nc.Block())

        flat = lambda t: t[:, :, :].rearrange("p a n -> p (a n)")
        pieces = []
        for src, hi, lo, n in ((w1, flat(W1h), flat(W1l), K * 3 * D), (wr, flat(Wrh), flat(Wrl), K * 3 * D),
                               (wk, flat(Wkh), flat(Wkl), K * 3 * D),
                               (ew1, flat(E1h), flat(E1l), (E + 1) * K * HID),
                               (ew2, flat(E2h), flat(E2l), (E + 1) * FC * D)):
            for a in range(0, n, STAGE):
                m = min(STAGE, n - a)
                pieces.append((src[:, a:a + m], hi[:, a:a + m], lo[:, a:a + m], m))
        stage_u0 = pre[:, 0:K * 3 * D]
        stage_w0 = pre[:, K * 3 * D:2 * K * 3 * D]
        stage_c0 = stage[:, :, :].rearrange("p s n -> p (s n)")[:, 0:K * 3 * D].rearrange("p (k n) -> p k n", k=K)

        @block.sync
        def _(sp):
            sp.dma_start(stage_w0, w0).then_inc(in_w0, 16)
            for i in range(N_TILES):
                cols = slice(i * NT, (i + 1) * NT)
                sp.dma_start(X[:, :, cols], xT[:, :, cols]).then_inc(in_x[i], 16)
                if i == 0:
                    for dst, src in ((cond[:, :, :], condT), (b0s[:, :], b0), (I[:, :], ident)):
                        sp.dma_start(dst, src).then_inc(in_small, 16)
                    sp.dma_start(stage_c0, c0).then_inc(in_small, 16)
                    sp.dma_start(stage_u0, u0).then_inc(in_u0, 16)
            for dst, src in ((b1s[:, :], b1), (eb1s[:, :], eb1), (eb2s[:, :], eb2), (gws[:, :, :], gate_w),
                             (tws[:, :, :], time_w), (sbb[:, :], small_b), (low[:, :], lower), (bs[:, :], bsel),
                             (mtok[:, :, :], mask_tok), (mcol[:, :], mask_col)):
                sp.dma_start(dst, src).then_inc(in_late, 16)
            sp.wait_ge(v_psum, 1)
            for n, (src, _, _, m) in enumerate(pieces):
                if n >= N_STAGE:
                    sp.wait_ge(stage_free, n - N_STAGE + 1)
                sp.dma_start(stage[:, n % N_STAGE, 0:m], src).then_inc(staged[n % N_STAGE], 16)
            with sp.Fori(0, N_TILES) as st:
                for s in range(SUB):
                    sp.wait_ge(out_ready, st * SUB + (s + 1))
                    sp.dma_start(out[:, bass.ds(st * TT + s * (P // B), P // B), :].rearrange("b t d -> t b d"),
                                 ACC[:, s, :]).then_inc(out_done, 16)
            sp.wait_ge(out_done, 16 * N_TILES * SUB + 16)

        @block.gpsimd
        def _(pool):
            for n, (_, hi, lo, m) in enumerate(pieces):
                src = stage[:, n % N_STAGE, 0:m]
                pool.wait_ge(staged[n % N_STAGE], 16 * (n // N_STAGE + 1))
                nc.gpsimd.tensor_scalar(src, src, SPLIT_SCALE, 1.0, ALU.mult, ALU.mult).then_inc(pool_step, 1)
                pool.wait_ge(pool_step, 2 * n + 1)
                if n == WK_PIECE:
                    pool.wait_ge(p0_psum, N_TILES * 3 * K)
                nc.gpsimd.tensor_copy(hi, src).then_inc(pool_step, 1)
                pool.wait_ge(pool_step, 2 * n + 2)
                nc.gpsimd.tensor_tensor(lo, src, hi, ALU.subtract).then_inc(stage_free, 1)

        def products(out_ap, wh, wl, ah, al, m, start):
            cols = slice(m * P, (m + 1) * P)
            for k in range(K):
                for n, (w, a) in enumerate(((wh, ah), (wl, ah), (wh, al))):
                    last = nc.tensor.matmul(out_ap, w[:, k, cols], a[:, k], start=start and k == 0 and n == 0,
                                            stop=k == K - 1 and n == 2)
            return last

        def halves(t):
            return t[:, :].rearrange("p (k b) -> p k b", k=K)

        def gate_products(psum, wh, wl, a, gate, part):
            last = None
            for m in range(K):
                for k in range(K):
                    cols = slice((gate * K + m) * P, (gate * K + m + 1) * P)
                    for w in ((wh, wl) if part == "hi" else (wh,)):
                        last = nc.tensor.matmul(psum[:, m * B:(m + 1) * B], w[:, k, cols], a[:, k * B:(k + 1) * B],
                                                start=False, stop=part == "lo" and m == K - 1 and k == K - 1,
                                                skip_group_check=True)
            return last

        def seed(psum, t, gate):
            for n, part in enumerate((PREh, PREl)):
                src = part[:, bass.ds(t, 1), gate * K * B:(gate + 1) * K * B].rearrange("p t c -> p (t c)")
                nc.tensor.matmul(psum[:, 0:K * B], I64[:, :], src, start=n == 0, stop=False, skip_group_check=True)

        @block.tensor
        def _(pe):
            pe.wait_ge(in_small, 64)
            for g in range(3 * K):
                for k in range(K):
                    last = nc.tensor.matmul(bank[7][:, g * B:(g + 1) * B], stage_c0[:, k, g * P:(g + 1) * P],
                                            cond[:, k, :], start=k == 0, stop=k == K - 1)
            last.then_inc(v_psum, 1)
            pe.wait_ge(w0_ready, 1)
            for i in range(N_TILES):
                pe.wait_ge(x0_split, i + 1)
                for g in range(3 * K):
                    n = i * 3 * K + g
                    if n >= 2:
                        pe.wait_ge(p0_free, n - 1)
                    cols = slice(i * NT, (i + 1) * NT)
                    products(bank[n % 2][:, :], W0h, W0l, Xh[:, :, cols], Xl[:, :, cols], g, True).then_inc(p0_psum, 1)
            R, Z, H = bank[2], bank[3], bank[4]
            pe.wait_ge(p0_free, N_TILES * 3 * K)
            pe.wait_ge(u0_ready, 1)
            with pe.Fori(0, T - UNROLL + 1, UNROLL) as t0:
                for u in range(UNROLL):
                    t = t0 + u
                    seed(R, t, 0)
                    seed(Z, t, 1)
                    pe.wait_ge(h_hi_ready, t + 1)
                    gate_products(R, U0h, U0l, hh_, 0, "hi")
                    pe.wait_ge(h_lo_ready, t + 1)
                    gate_products(R, U0h, U0l, hl_, 0, "lo").then_inc(r_psum, 1)
                    gate_products(Z, U0h, U0l, hh_, 1, "hi")
                    gate_products(Z, U0h, U0l, hl_, 1, "lo").then_inc(z_psum, 1)
                    seed(H, t, 2)
                    pe.wait_ge(rh_hi_ready, t + 1)
                    gate_products(H, U0h, U0l, rhh, 2, "hi")
                    pe.wait_ge(rh_lo_ready, t + 1)
                    gate_products(H, U0h, U0l, rhl, 2, "lo").then_inc(hh_psum, 1)
                    pe.wait_ge(z_sig, t + 1)
            pe.wait_ge(stage_free, 2)
            for i in range(N_TILES):
                pe.wait_ge(x1_split, i + 1)
                for g in range(3 * K):
                    n = i * 3 * K + g
                    if n >= 2:
                        pe.wait_ge(p1_free, n - 1)
                    cols = slice(i * NT, (i + 1) * NT)
                    products(bank[n % 2][:, :], W1h, W1l, Xh[:, :, cols], Xl[:, :, cols], g, True).then_inc(p1_psum, 1)
            pe.wait_ge(stage_free, 6)
            for i in range(N_TILES):
                pe.wait_ge(x2_split, i + 1)
                for g in range(3 * K):
                    n = i * 3 * K + g
                    if n >= 2:
                        pe.wait_ge(p2_free, n - 1)
                    cols = slice(i * NT, (i + 1) * NT)
                    products(bank[n % 2][:, :], Wkh, Wkl, Xh[:, :, cols], Xl[:, :, cols], g, True).then_inc(p2_psum, 1)
            Fb, Ob, Gb = bank[2], bank[3], bank[4]
            pe.wait_ge(p2_free, N_TILES * 3 * K)
            with pe.Fori(0, T - UNROLL + 1, UNROLL) as t0:
                for u in range(UNROLL):
                    t = t0 + u
                    seed(Gb, t, 2)
                    seed(Fb, t, 0)
                    seed(Ob, t, 1)
                    pe.wait_ge(s_hi_ready, t + 1)
                    gate_products(Gb, Wrh, Wrl, hh_, 2, "hi")
                    pe.wait_ge(s_lo_ready, t + 1)
                    gate_products(Gb, Wrh, Wrl, hl_, 2, "lo").then_inc(g_psum, 1)
                    gate_products(Fb, Wrh, Wrl, hh_, 0, "hi")
                    gate_products(Fb, Wrh, Wrl, hl_, 0, "lo").then_inc(f_psum, 1)
                    gate_products(Ob, Wrh, Wrl, hh_, 1, "hi")
                    gate_products(Ob, Wrh, Wrl, hl_, 1, "lo").then_inc(o_psum, 1)
                    pe.wait_ge(o_sig, t + 1)
            pe.wait_ge(in_late, 160)
            pe.wait_ge(silu_ready, 1)
            for k in range(K):
                nc.tensor.matmul(bank[7][0:B, 0:2 * E], silu[:, k, :], tws[:, k, :], start=k == 0, stop=k == K - 1)
            pe.wait_ge(agg_ready, 1)
            for a in range(3):
                for k in range(K):
                    last = nc.tensor.matmul(bank[6][0:B, 0:E], agg[:, a, k * B:(k + 1) * B], gws[:, a * K + k, :],
                                            start=a == 0 and k == 0, stop=a == 2 and k == K - 1)
            last.then_inc(gate_psum, 1)
            pe.wait_ge(sel_ready, 1)
            nc.tensor.matmul(bank[7][:, 0:E], bs[:, :], sel5[:, 0:E], start=True, stop=True)
            nc.tensor.matmul(bank[6][0:E + 1, 0:P], sel5[:, :], bs[:, :], start=True, stop=True).then_inc(wsel_psum, 1)
            pe.wait_ge(w_ready, 1)
            pe.wait_ge(stage_free, len(pieces))

            def up(st, n):
                e, f = divmod(n, FC)
                if n >= 2:
                    pe.wait_ge(gelu_ready, st * N_BLOCKS + (n - 1))
                for k in range(K):
                    cols = slice(k * HID + f * P, k * HID + (f + 1) * P)
                    for j, (w, a) in enumerate(((E1h, Xh), (E1l, Xh), (E1h, Xl))):
                        last = nc.tensor.matmul(bank[n % 2][:, :], w[:, e, cols], a[:, k, bass.ds(st * NT, NT)],
                                                start=k == 0 and j == 0, stop=k == K - 1 and j == 2)
                last.then_inc(up_psum, 1)

            def down(st, n):
                e, f = divmod(n, FC)
                if f == 0:
                    pe.wait_ge(y_free, st * ((E + 1) * SUB) + (e * SUB + 1))
                pe.wait_ge(gh_ready, st * N_BLOCKS + (n + 1))
                for part, weights in ((Gh, (E2h, E2l)), (Gl, (E2h,))):
                    if part is Gl:
                        pe.wait_ge(gl_ready, st * N_BLOCKS + (n + 2))
                    for s in range(SUB):
                        for w in weights:
                            last = nc.tensor.matmul(bank[2 + s][:, 0:D], part[:, n % 2, s * P:(s + 1) * P],
                                                    w[:, e, f * D:(f + 1) * D], start=f == 0 and w is E2h and part is Gh,
                                                    stop=False, skip_group_check=True)
                last.then_inc(down_done, 1)

            def residual(st):
                for s in range(SUB):
                    tok = bass.ds(st * NT + s * P, P)
                    for k in range(K):
                        for part in (Xh, Xl):
                            nc.tensor.matmul(bank[2 + s][:, k * P:(k + 1) * P], part[:, k, tok], I64[:, :],
                                             start=False, stop=False, skip_group_check=True)
                    for w, eb in ((wcolh, eb2h), (wcoll, eb2h), (wcolh, eb2l)):
                        nc.tensor.matmul(bank[2 + s][:, 0:D], w[:, tok], eb[:, :], start=False, stop=False,
                                         skip_group_check=True)

            with pe.Fori(0, N_TILES) as st:
                up(st, 0)
                for n in range(N_BLOCKS):
                    if n + 1 < N_BLOCKS:
                        up(st, n + 1)
                    if n == N_BLOCKS - 1:
                        residual(st)
                    down(st, n)

        def tile_view(ap):
            return ap.rearrange("p (t b) -> p t b", b=B)

        @block.scalar
        def _(act):
            nc.scalar.preload_act_table(ACT.Sigmoid)
            with act.Fori(0, T - UNROLL + 1, UNROLL) as t0:
                for u in range(UNROLL):
                    t = t0 + u
                    act.wait_ge(r_psum, t + 1)
                    nc.scalar.activation(gr[:, :], bank[2][:, 0:K * B], ACT.Sigmoid, scale=UNSCALE).then_inc(r_sig, 1)
                    act.wait_ge(z_psum, t + 1)
                    nc.scalar.activation(gz[:, :], bank[3][:, 0:K * B], ACT.Sigmoid, scale=UNSCALE).then_inc(z_sig, 1)
                    act.wait_ge(hh_psum, t + 1)
                    nc.scalar.activation(gh[:, :], bank[4][:, 0:K * B], ACT.Tanh, scale=UNSCALE).then_inc(hh_tanh, 1)
            act.wait_ge(in_late, 160)
            for i in range(N_TILES):
                for g in range(3 * K):
                    n = i * 3 * K + g
                    act.wait_ge(p1_psum, n + 1)
                    dst = (bufA, bufB, bufC)[g // K][:, g % K, i * NT:(i + 1) * NT]
                    nc.scalar.activation(dst, bank[n % 2][:, :], ACT.Sigmoid if g < 2 * K else ACT.Identity,
                                         bias=b1s[:, g:g + 1], scale=UNSCALE).then_inc(p1_free, 1)
            nc.scalar.activation(sgc[:, :, :], cond[:, :, :], ACT.Sigmoid).then_inc(sgc_ready, 1)
            act.wait_ge(norm1, 1)
            nc.scalar.activation(bufA[:, :, :], bufA[:, :, :], ACT.Ln, bias=eps[:, 0:1]).then_inc(logs1, 1)
            act.wait_ge(lc1, K * B)
            nc.scalar.activation(bufA[:, :, 0:B], bufC[:, :, TOK - B:TOK], ACT.Exp).then_inc(exps1, 1)
            for k in range(K):
                for b in range(B):
                    nc.scalar.activation(tile_view(bufA[:, k, :])[:, 1:T, b], tile_view(bufC[:, k, :])[:, 0:T - 1, b],
                                         ACT.Exp, bias=bufC[:, k, TOK - B + b:TOK - B + b + 1], scale=-1.0)\
                        .then_inc(exps1, 1)
            nc.scalar.activation(bufD[:, :, :], bufC[:, :, :], ACT.Exp).then_inc(elc1, 1)
            for n in range(N_TILES * 3 * K):
                i, g = divmod(n, 3 * K)
                act.wait_ge(p2_psum, n + 1)
                nc.scalar.activation(PREh[:, i * TT:(i + 1) * TT, g * B:(g + 1) * B], tile_view(bank[n % 2][:, :]),
                                     ACT.Identity, scale=UNSCALE).then_inc(p2_hi, 1)
            nc.scalar.preload_act_table(ACT.Sigmoid)
            with act.Fori(0, T - UNROLL + 1, UNROLL) as t0:
                for u in range(UNROLL):
                    t = t0 + u
                    act.wait_ge(g_psum, t + 1)
                    nc.scalar.activation(gh[:, :], bank[4][:, 0:K * B], ACT.Tanh, scale=UNSCALE).then_inc(g_tanh, 1)
                    act.wait_ge(f_psum, t + 1)
                    nc.scalar.activation(gr[:, :], bank[2][:, 0:K * B], ACT.Sigmoid, scale=UNSCALE).then_inc(f_sig, 1)
                    act.wait_ge(o_psum, t + 1)
                    nc.scalar.activation(gz[:, :], bank[3][:, 0:K * B], ACT.Sigmoid, scale=UNSCALE).then_inc(o_sig, 1)
                    act.wait_ge(c_ready, t + 2)
                    nc.scalar.activation(tcell[:, :], cell[:, :], ACT.Tanh).then_inc(c_tanh, 1)
            act.wait_ge(mx_ready, 1)
            nc.scalar.activation(ex[:, :], lg[:, :], ACT.Exp, bias=mx[:, 0:1]).then_inc(ex_ready, 1)
            nc.scalar.preload_act_table(ACT.Gelu_apprx_tanh)
            with act.Fori(0, N_TILES) as st:
                for n in range(N_BLOCKS):
                    act.wait_ge(up_psum, st * N_BLOCKS + (n + 1))
                    if n >= 2:
                        act.wait_ge(gl_ready, st * N_BLOCKS + n)
                    else:
                        act.wait_ge(gl_ready, st * N_BLOCKS + 1)
                    nc.scalar.activation(G[:, n % 2, :], bank[n % 2][:, :], ACT.Gelu_apprx_tanh,
                                         bias=eb1s[:, n:n + 1], scale=UNSCALE).then_inc(gelu_ready, 1)

        @block.vector
        def _(dve):
            steps = [0]

            def then_wait(ins):
                steps[0] += 1
                ins.then_inc(dve_step, 1)
                dve.wait_ge(dve_step, steps[0])

            def split(src, hi, lo, done, scale=None):
                if scale is None:
                    then_wait(nc.vector.tensor_copy(hi, src))
                    nc.vector.tensor_tensor(lo, src, hi, ALU.subtract).then_inc(done, 1)
                else:
                    then_wait(nc.vector.tensor_scalar(hi, src, scale, None, ALU.mult))
                    nc.vector.scalar_tensor_tensor(lo, src, scale, hi, ALU.mult, ALU.subtract).then_inc(done, 1)

            nc.vector.memset(zeros[:, :], 0.0)
            nc.vector.memset(eps[:, :], EPS).then_inc(dve_step, 1)
            steps[0] += 1
            for n, (begun, count) in enumerate(((x1_added, 1), (x3_added, 1), (gl_ready, 1), (down_done, 1),
                                                (y_free, 1), (out_done, 16))):
                nc.vector.memset(mark[:, n:n + 1], 0.0).then_inc(begun, count)
            nc.vector.memset(h32[:, :], 0.0).then_inc(h_32_ready, 1)
            nc.vector.memset(hh_[:, :], 0.0).then_inc(h_hi_ready, 1)
            nc.vector.memset(hl_[:, :], 0.0).then_inc(h_lo_ready, 1)
            dve.wait_ge(in_w0, 16)
            split(stage_w0, flat(W0h), flat(W0l), w0_ready, SPLIT_SCALE)
            for i in range(N_TILES):
                dve.wait_ge(in_x[i], 16)
                cols = slice(i * NT, (i + 1) * NT)
                split(X[:, :, cols], Xh[:, :, cols], Xl[:, :, cols], x0_split)
                if i == 0:
                    dve.wait_ge(in_u0, 16)
                    split(stage_u0, flat(U0h), flat(U0l), u0_ready, SPLIT_SCALE)
            dve.wait_ge(in_small, 64)
            nc.vector.tensor_scalar(I64[:, :], I[:, :], SPLIT_SCALE, None, ALU.mult).then_inc(v_ready, 1)
            dve.wait_ge(v_psum, 1)
            then_wait(nc.vector.tensor_tensor(v0[:, :, :], bank[7][:, 0:3 * K * B].rearrange("p (g b) -> p g b", b=B),
                                              b0s[:, :, None].broadcast_to([P, 3 * K, B]), ALU.add))
            dve.wait_ge(u0_ready, 1)
            for n in range(N_TILES * 3 * K):
                i, g = divmod(n, 3 * K)
                hi = PREh[:, i * TT:(i + 1) * TT, g * B:(g + 1) * B]
                lo = PREl[:, i * TT:(i + 1) * TT, g * B:(g + 1) * B]
                v = v0[:, g:g + 1, :].broadcast_to([P, TT, B])
                dve.wait_ge(p0_psum, n + 1)
                nc.vector.scalar_tensor_tensor(hi, tile_view(bank[n % 2][:, :]), UNSCALE, v, ALU.mult, ALU.add)
                if n:
                    dve.wait_ge(p0_free, n)
                then_wait(nc.vector.scalar_tensor_tensor(tile_view(preproj[:, :]), tile_view(bank[n % 2][:, :]),
                                                         UNSCALE, v, ALU.mult, ALU.add))
                nc.vector.tensor_tensor(lo, tile_view(preproj[:, :]), hi, ALU.subtract).then_inc(p0_free, 1)

            with dve.Fori(0, T - UNROLL + 1, UNROLL) as t0:
                for u in range(UNROLL):
                    t = t0 + u
                    dve.wait_ge(r_sig, t + 1)
                    nc.vector.tensor_tensor(rhh[:, :], gr[:, :], h32[:, :], ALU.mult).then_inc(rh_hi_ready, 1)
                    nc.vector.tensor_tensor(rh32[:, :], gr[:, :], h32[:, :], ALU.mult).then_inc(rh_32_ready, 1)
                    dve.wait_ge(rh_32_ready, t + 1)
                    nc.vector.tensor_tensor(rhl[:, :], rh32[:, :], rhh[:, :], ALU.subtract).then_inc(rh_lo_ready, 1)
                    dve.wait_ge(z_sig, t + 1)
                    nc.vector.scalar_tensor_tensor(nah[:, :], gz[:, :], 1.0, h32[:, :], ALU.subtract, ALU.mult)\
                        .then_inc(nah_ready, 1)
                    dve.wait_ge(hh_tanh, t + 1)
                    nc.vector.tensor_tensor(zh[:, :], gz[:, :], gh[:, :], ALU.mult).then_inc(zh_ready, 1)
                    dve.wait_ge(zh_ready, t + 1)
                    nc.vector.tensor_tensor(hh_[:, :], zh[:, :], nah[:, :], ALU.subtract).then_inc(h_hi_ready, 1)
                    dve.wait_ge(x1_added, t + 1)
                    nc.vector.tensor_tensor(h32[:, :], zh[:, :], nah[:, :], ALU.subtract).then_inc(h_32_ready, 1)
                    dve.wait_ge(h_32_ready, t + 2)
                    nc.vector.tensor_tensor(hl_[:, :], h32[:, :], hh_[:, :], ALU.subtract).then_inc(h_lo_ready, 1)
                    xs = X[:, :, bass.ds(t * B, B)]
                    nc.vector.tensor_tensor(xs, xs, halves(h32), ALU.add).then_inc(x1_added, 1)

            dve.wait_ge(x1_added, T + 1)
            for i in range(N_TILES):
                cols = slice(i * NT, (i + 1) * NT)
                split(X[:, :, cols], Xh[:, :, cols], Xl[:, :, cols], x1_split)
            dve.wait_ge(p1_free, N_TILES * 3 * K)
            A_, B_, C_, D_ = (x[:, :, :] for x in (bufA, bufB, bufC, bufD))
            then_wait(nc.vector.scalar_tensor_tensor(D_, A_, EPS, B_, ALU.add, ALU.add))
            then_wait(nc.vector.reciprocal(D_, D_))
            nc.vector.tensor_tensor(A_, A_, D_, ALU.mult).then_inc(norm1, 1)
            then_wait(nc.vector.tensor_tensor(B_, B_, D_, ALU.mult))
            then_wait(nc.vector.tensor_tensor(B_, B_, C_, ALU.mult))

            def cumsum(dst, src, done):
                for k in range(K):
                    for b in range(B):
                        nc.vector.tensor_tensor_scan(tile_view(dst[:, k, :])[:, :, b], tile_view(src[:, k, :])[:, :, b],
                                                     zeros[:, :], 0.0, ALU.add, ALU.add).then_inc(done, 1)

            dve.wait_ge(logs1, 1)
            cumsum(bufC, bufA, lc1)
            dve.wait_ge(exps1, 1 + K * B)
            then_wait(nc.vector.tensor_tensor(B_, B_, A_, ALU.mult))
            cumsum(bufA, bufB, lc1)
            dve.wait_ge(elc1, 1)
            for k in range(K):
                d = tile_view(bufD[:, k, :])
                ins = nc.vector.tensor_tensor(d, d, cond[:, k:k + 1, :].broadcast_to([P, T, B]), ALU.mult)
            dve.wait_ge(lc1, 2 * K * B)
            then_wait(ins)
            then_wait(nc.vector.tensor_tensor(A_, A_, D_, ALU.add))
            then_wait(nc.vector.tensor_tensor(X[:, :, :], X[:, :, :], A_, ALU.add))

            for i in range(N_TILES):
                cols = slice(i * NT, (i + 1) * NT)
                split(X[:, :, cols], Xh[:, :, cols], Xl[:, :, cols], x2_split)
            dve.wait_ge(sgc_ready, 1)
            nc.vector.tensor_tensor(silu[:, :, :], sgc[:, :, :], cond[:, :, :], ALU.mult).then_inc(silu_ready, 1)
            for n in range(N_TILES * 3 * K):
                i, g = divmod(n, 3 * K)
                dve.wait_ge(p2_hi, n + 1)
                nc.vector.scalar_tensor_tensor(PREl[:, i * TT:(i + 1) * TT, g * B:(g + 1) * B], tile_view(bank[n % 2][:, :]),
                                               UNSCALE, PREh[:, i * TT:(i + 1) * TT, g * B:(g + 1) * B],
                                               ALU.mult, ALU.subtract).then_inc(p2_free, 1)
            nc.vector.tensor_copy(halves(cell), cond[:, :, :]).then_inc(c_ready, 1)
            nc.vector.tensor_copy(halves(hh_), cond[:, :, :]).then_inc(s_hi_ready, 1)
            dve.wait_ge(s_hi_ready, 1)
            nc.vector.tensor_tensor(halves(hl_), cond[:, :, :], halves(hh_), ALU.subtract).then_inc(s_lo_ready, 1)
            with dve.Fori(0, T - UNROLL + 1, UNROLL) as t0:
                for u in range(UNROLL):
                    t = t0 + u
                    dve.wait_ge(c_ready, t + 1)
                    dve.wait_ge(g_tanh, t + 1)
                    nc.vector.tensor_tensor(nah[:, :], cell[:, :], gh[:, :], ALU.subtract).then_inc(d_ready, 1)
                    dve.wait_ge(d_ready, t + 1)
                    dve.wait_ge(f_sig, t + 1)
                    nc.vector.tensor_tensor(zh[:, :], gr[:, :], nah[:, :], ALU.mult).then_inc(m_ready, 1)
                    dve.wait_ge(m_ready, t + 1)
                    nc.vector.tensor_tensor(cell[:, :], zh[:, :], gh[:, :], ALU.add).then_inc(c_ready, 1)
                    dve.wait_ge(o_sig, t + 1)
                    dve.wait_ge(c_tanh, t + 1)
                    nc.vector.tensor_tensor(hh_[:, :], gz[:, :], tcell[:, :], ALU.mult).then_inc(s_hi_ready, 1)
                    dve.wait_ge(x3_added, t + 1)
                    nc.vector.tensor_tensor(h32[:, :], gz[:, :], tcell[:, :], ALU.mult).then_inc(s_32_ready, 1)
                    dve.wait_ge(s_32_ready, t + 1)
                    nc.vector.tensor_tensor(hl_[:, :], h32[:, :], hh_[:, :], ALU.subtract).then_inc(s_lo_ready, 1)
                    xs = X[:, :, bass.ds(t * B, B)]
                    nc.vector.tensor_tensor(xs, xs, halves(h32), ALU.add).then_inc(x3_added, 1)

            dve.wait_ge(x3_added, T + 1)
            for i in range(N_TILES):
                cols = slice(i * NT, (i + 1) * NT)
                split(X[:, :, cols], Xh[:, :, cols], Xl[:, :, cols], x3_split)
            for k in range(K):
                for s, (a, z) in enumerate(((0, L_HEAD), (L_HEAD, 2 * L_HEAD), (2 * L_HEAD, T))):
                    ins = nc.vector.tensor_reduce(seg[:, s, k * B:(k + 1) * B],
                                                  X[:, k, a * B:z * B].rearrange("p (t b) -> p b t", b=B),
                                                  AX_X, ALU.add)
            dve.wait_ge(in_late, 160)
            then_wait(ins)
            nc.vector.tensor_tensor(agg[:, 1, :], seg[:, 0, :], seg[:, 2, :], ALU.add)
            then_wait(nc.vector.tensor_tensor(agg[:, 2, :], seg[:, 1, :], seg[:, 2, :], ALU.add))
            then_wait(nc.vector.tensor_tensor(agg[:, 0, :], agg[:, 1, :], seg[:, 1, :], ALU.add))
            nc.vector.tensor_scalar(agg[:, 0, :], agg[:, 0, :], 1.0 / T, None, ALU.mult)
            nc.vector.tensor_scalar(agg[:, 1:3, :], agg[:, 1:3, :], 1.0 / (L_HEAD + L_PROPRIO), None, ALU.mult)\
                .then_inc(agg_ready, 1)
            dve.wait_ge(gate_psum, 1)
            then_wait(nc.vector.tensor_tensor(mod[:, :], bank[7][0:B, 0:2 * E], sbb[:, E:3 * E], ALU.add))
            then_wait(nc.vector.tensor_tensor(lg[:, :], bank[6][0:B, 0:E], sbb[:, 0:E], ALU.add))
            then_wait(nc.vector.scalar_tensor_tensor(lg[:, :], mod[:, 0:E], 1.0, lg[:, :], ALU.add, ALU.mult))
            then_wait(nc.vector.tensor_tensor(lg[:, :], lg[:, :], mod[:, E:2 * E], ALU.add))
            then_wait(nc.vector.reduce_max(mx[:, :], lg[:, :], AX_X))
            nc.vector.tensor_scalar(mx[:, :], mx[:, :], -1.0, None, ALU.mult).then_inc(mx_ready, 1)
            dve.wait_ge(ex_ready, 1)
            then_wait(nc.vector.reduce_sum(sm[:, :], ex[:, :], AX_X))
            then_wait(nc.vector.reciprocal(rs[:, :], sm[:, :]))
            then_wait(nc.vector.tensor_scalar(sc[:, :], ex[:, :], rs[:, 0:1], None, ALU.mult))
            scj = sc[:, None, :].broadcast_to([B, E, E])
            sce = sc[:, :, None].broadcast_to([B, E, E])
            then_wait(nc.vector.tensor_tensor(g3[:, :, :], scj, sce, ALU.is_gt))
            then_wait(nc.vector.tensor_tensor(q3[:, :, :], scj, sce, ALU.is_equal))
            then_wait(nc.vector.tensor_tensor(q3[:, :, :], q3[:, :, :], low[:, :].rearrange("p (e j) -> p e j", e=E), ALU.mult))
            then_wait(nc.vector.tensor_tensor(g3[:, :, :], g3[:, :, :], q3[:, :, :], ALU.add))
            then_wait(nc.vector.reduce_sum(rank[:, :], g3[:, :, :], AX_X))
            then_wait(nc.vector.scalar_tensor_tensor(sel5[:, 0:E], rank[:, :], 1.5, sc[:, :], ALU.is_lt, ALU.mult))
            then_wait(nc.vector.reduce_sum(sm[:, :], sel5[:, 0:E], AX_X))
            then_wait(nc.vector.tensor_scalar(sm[:, :], sm[:, :], EPS, None, ALU.add))
            then_wait(nc.vector.reciprocal(rs[:, :], sm[:, :]))
            then_wait(nc.vector.tensor_scalar(sel5[:, 0:E], sel5[:, 0:E], rs[:, 0:1], None, ALU.mult))
            nc.vector.memset(sel5[:, E:E + 1], 1.0).then_inc(sel_ready, 1)
            dve.wait_ge(wsel_psum, 1)
            wp = bank[7][:, None, 0:E].broadcast_to([P, TOK // P, E])
            nc.vector.tensor_tensor(wtok[:, :, :], wp, mtok[:, :, :], ALU.mult)
            then_wait(nc.vector.tensor_copy(wc[:, :], bank[6][0:E + 1, 0:P]))
            then_wait(nc.vector.tensor_copy(wch[:, :], wc[:, :]))
            then_wait(nc.vector.tensor_tensor(wcl[:, :], wc[:, :], wch[:, :], ALU.subtract))
            for src, dst in ((wch, wcolh), (wcl, wcoll)):
                nc.vector.tensor_tensor(dst.rearrange("p (a n) -> p a n", n=P),
                                        src[:, None, :].broadcast_to([E + 1, TOK // P, P]),
                                        mcol[:, :].rearrange("p (a n) -> p a n", n=P), ALU.mult)
            split(eb2s[:, :], eb2h[:, :], eb2l[:, :], w_ready, SPLIT_SCALE)

            def expert_rows(st, e):
                dve.wait_ge(down_done, st * N_BLOCKS + ((e + 1) * FC + 1))
                if e == 0:
                    dve.wait_ge(out_done, st * (16 * SUB) + 16)
                else:
                    dve.wait_ge(y_free, st * ((E + 1) * SUB) + (e * SUB + 1))
                for s in range(SUB):
                    rows, acc = bank[2 + s][:, 0:D], ACC[:, s, :]
                    w = wtok[:, bass.ds(st * SUB + s, 1), min(e, E - 1)]
                    if e == 0:
                        nc.vector.tensor_scalar(acc, rows, w, None, ALU.mult).then_inc(y_free, 1)
                    elif e < E:
                        nc.vector.scalar_tensor_tensor(acc, rows, w, acc, ALU.mult, ALU.add).then_inc(y_free, 1)
                    else:
                        nc.vector.scalar_tensor_tensor(acc, rows, UNSCALE, acc, ALU.mult, ALU.add).then_inc(y_free, 1)
                if e == E:
                    dve.wait_ge(y_free, st * ((E + 1) * SUB) + ((E + 1) * SUB + 1))
                    nc.vector.memset(mark[:, 7:8], 0.0).then_inc(out_ready, SUB)

            with dve.Fori(0, N_TILES) as st:
                for n in range(N_BLOCKS):
                    dve.wait_ge(gelu_ready, st * N_BLOCKS + (n + 1))
                    dve.wait_ge(down_done, st * N_BLOCKS + max(n, 1))
                    nc.vector.tensor_copy(Gh[:, n % 2, :], G[:, n % 2, :]).then_inc(gh_ready, 1)
                    dve.wait_ge(gh_ready, st * N_BLOCKS + (n + 1))
                    nc.vector.tensor_tensor(Gl[:, n % 2, :], G[:, n % 2, :], Gh[:, n % 2, :], ALU.subtract)\
                        .then_inc(gl_ready, 1)
                    if n % FC == 0 and n:
                        expert_rows(st, n // FC - 1)
                expert_rows(st, E)


def kernel(**inputs):
    import numpy as np
    import concourse.bacc as bacc
    from concourse.bass_utils import run_bass_kernel_spmd as run

    g = {n: np.asarray(a) for n, a in inputs.items()}

    def halves_first(w):
        return w.reshape(K, P, -1).transpose(1, 0, 2)

    def columns(*bs):
        return np.concatenate(bs).reshape(-1, P).T

    def gates(*ws):
        return halves_first(np.concatenate(ws, axis=1)).reshape(P, -1)

    c = lambda n: g["L0_cond_" + n]
    f = lambda n: g["L1_cond_" + n]
    m = lambda n: g["L3_cond_" + n]
    t = np.arange(T)
    mask = np.ones((E, T), np.float32)
    mask[1, L_HEAD:2 * L_HEAD] = 0.0
    mask[2, :L_HEAD] = 0.0
    by_row = mask.reshape(E, TOK // P, P // B, 1).repeat(B, axis=3).reshape(E, TOK // P, P)
    arrays = {
        "xT": g["x"].transpose(2, 1, 0).reshape(K, P, TOK).transpose(1, 0, 2),
        "condT": halves_first(g["cond_1024"].T),
        "w0": gates(c("W_r"), c("W_z"), c("W")),
        "u0": gates(c("U_r"), c("U_z"), c("U")),
        "c0": gates(c("C_r"), c("C_z"), c("C")).reshape(P, K, 3 * D),
        "b0": columns(c("b_r"), c("b_z"), c("b")),
        "w1": gates(f("W_f").T, f("W_i").T, f("W_h").T),
        "b1": columns(f("b_f"), f("b_i"), f("b_h")),
        "wk": gates(g["L2_cond_Wk"]),
        "wr": gates(g["L2_cond_Wr"]),
        "gate_w": m("gate_w").reshape(3 * K, P, E).transpose(1, 0, 2),
        "time_w": halves_first(m("time_w")),
        "small_b": np.broadcast_to(np.concatenate([m("gate_b"), m("time_b")]), (B, 3 * E)),
        "eb1": columns(m("eb1").ravel(), m("sb1")),
        "eb2": np.concatenate([m("eb2"), m("sb2")[None]]),
        "ew1": np.concatenate([m("ew1"), m("sw1")[None]]).reshape(E + 1, K, P, HID).transpose(2, 0, 1, 3).reshape(P, -1),
        "ew2": np.concatenate([m("ew2"), m("sw2")[None]]).reshape(E + 1, FC, P, D).transpose(2, 0, 1, 3).reshape(P, -1),
        "ident": np.eye(P, dtype=np.float32),
        "bsel": (np.arange(P)[None] % B == np.arange(B)[:, None]).astype(np.float32),
        "lower": np.broadcast_to(np.tril(np.ones((E, E), np.float32), -1).reshape(1, E * E), (B, E * E)),
        "mask_tok": by_row.transpose(2, 1, 0) * np.float32(UNSCALE),
        "mask_col": np.concatenate([by_row.reshape(E, TOK), np.ones((1, TOK), np.float32)]).astype(np.float16),
    }
    nc = bacc.Bacc("TRN2", target_bir_lowering=False, num_devices=1)
    arrays = {n: np.ascontiguousarray(a) for n, a in arrays.items()}
    aps = {n: nc.dram_tensor("in_" + n, a.shape, mybir.dt.from_np(a.dtype), kind="ExternalInput").ap()
           for n, a in arrays.items()}
    out = nc.dram_tensor("out_0", (B, T, D), F32, kind="ExternalOutput").ap()
    build(nc, **aps, out=out)
    r = run(nc, [{"in_" + n: a for n, a in arrays.items()}], core_ids=[0])
    return r.results[0]["out_0"]
```

```python
from contextlib import ExitStack

import concourse.bass as bass
from concourse import mybir

F32 = mybir.dt.float32
F16 = mybir.dt.float16
ACT = mybir.ActivationFunctionType
ALU = mybir.AluOpType
AX_X = mybir.AxisListType.X

P = 128
B, T, D = 8, 256, 256
K = D // P
TOK = B * T
SPLIT_SCALE = 64.0
UNSCALE = 1.0 / SPLIT_SCALE
EPS = 1e-8
E = 4
HID = 1024
FC = HID // P
N_BLOCKS = (E + 1) * FC
TS = 32
TC = TS * B
N_TILES3 = T // TS
SUB = TC // P
ROWS = TOK // P
CHUNK = 8
LAST_UP = TS - 2
NT = 512
TT = NT // B
N_TILES = TOK // NT
UNROLL = 8
L_HEAD = T // 3
L_PROPRIO = T - 2 * L_HEAD
CUTS = [0, *sorted((L_HEAD % TS, 2 * L_HEAD % TS)), TS]
STAGE = 1024
N_STAGE = 2
ROUTED = 12
IN_LATE = 16 * 9
WK_PIECE = 2 * -(-K * 3 * D // STAGE)


def build(nc, xT, condT, w0, u0, c0, b0, w1, b1, wk, wr, gate_w, time_w, small_b, eb1, eb2,
          ew1, ew2, ident, bsel, lower, mask_tok, out):
    with ExitStack() as ctx:
        def sb(name, shape, dt=F32):
            return ctx.enter_context(nc.sbuf_tensor(name, shape, dt))

        def sem(name):
            return ctx.enter_context(nc.semaphore(name))

        X = sb("X", [P, K, TOK])
        XS = sb("XS", [P, 2 * K * TOK], F16)
        XS_T = XS[:, :].rearrange("p (t c) -> p t c", c=2 * K * B)
        XS_n = XS[:, :].rearrange("p (i h k n) -> p i h k n", i=N_TILES3, h=2, k=K)
        bufD = XS[:, :].bitcast(F32).rearrange("p (k n) -> p k n", k=K)
        pre = sb("pre", [P, 3 * K * TOK])
        PRE = pre[:, :].bitcast(F16).rearrange("p (t c) -> p t c", c=6 * K * B)
        bufA, bufB, bufC = (pre[:, i * K * TOK:(i + 1) * K * TOK].rearrange("p (k n) -> p k n", k=K)
                            for i in range(3))
        PRE_Y = pre[:, :].rearrange("p (t c) -> p t c", c=3 * K * B)
        XS_Y = XS[:, :].bitcast(F32).rearrange("p (t c) -> p t c", c=K * B)
        preproj = sb("preproj", [P, NT])
        stage = sb("stage", [P, N_STAGE, STAGE])
        flat_stage = stage[:, :, :].rearrange("p s n -> p (s n)")
        W0h, W0l = sb("W0h", [P, K, 3 * D], F16), sb("W0l", [P, K, 3 * D], F16)
        G = flat_stage[:, 0:2 * TC].rearrange("p (s n) -> p s n", n=TC)
        Gh, Gl = (flat_stage[:, a * TC:(a + 2) * TC].bitcast(F16).rearrange("p (s n) -> p s n", n=TC) for a in (2, 4))
        U0h, U0l = sb("U0h", [P, K, 3 * D], F16), sb("U0l", [P, K, 3 * D], F16)
        W1 = sb("W1", [P, 2, K * 3 * D], F16)
        W1h, W1l = (W1[:, i, :].rearrange("p (k n) -> p k n", k=K) for i in range(2))
        SEEDS = W1[:, :, :].rearrange("p h n -> p (h n)").rearrange("p (t c) -> p t c", c=6 * K * B)
        Wkh, Wkl = W0h, W0l
        Wrh, Wrl = sb("Wrh", [P, K, 3 * D], F16), sb("Wrl", [P, K, 3 * D], F16)
        E1h, E1l = sb("E1h", [P, E + 1, K * HID], F16), sb("E1l", [P, E + 1, K * HID], F16)
        E2h, E2l = sb("E2h", [P, E + 1, FC * D], F16), sb("E2l", [P, E + 1, FC * D], F16)
        I = sb("I", [P, P], F32)
        I64 = sb("I64", [P, P], F16)
        cond = sb("cond", [P, K, B])
        v0 = sb("v0", [P, 3 * K, B])
        b0s = sb("b0s", [P, 3 * K])
        b1s = sb("b1s", [P, 3 * K])
        eb1s = sb("eb1s", [P, (E + 1) * FC])
        hh_ = sb("h_hi", [P, K * B], F16)
        hl_ = sb("h_lo", [P, K * B], F16)
        rhh, rhl, rh32 = sb("rh_hi", [P, K * B], F16), sb("rh_lo", [P, K * B], F16), sb("rh32", [P, K * B])
        gr, gz, gh = sb("gr", [P, K * B]), sb("gz", [P, K * B]), sb("gh", [P, K * B])
        fma_m, fma_ab = sb("fma_m", [P, K * B, 2]), sb("fma_ab", [P, K * B, 2])
        hs32, hs16 = sb("hs32", [P, 2, K * B, 2]), sb("hs16", [P, K * B, 2], F16)
        h32 = sb("h32", [P, 2, K * B])
        zeros, eps, mark = sb("zeros", [P, T]), sb("eps", [P, 1]), sb("mark", [P, 16])
        tcell = sb("tcell", [P, K * B])
        sgc, silu = sb("sgc", [P, K, B]), sb("silu", [P, K, B])
        gws = sb("gws", [P, 3 * K, E])
        tws = sb("tws", [P, K, 2 * E])
        sbb = sb("sbb", [B, 3 * E])
        part = sb("part", [P, T, 2])
        part9 = sb("part9", [P, 3, 3, K * B])
        seg = sb("seg", [P, 3, K * B])
        agg = sb("agg", [P, 3, K * B])
        lg, mod, ex, sc = sb("lg", [B, E]), sb("mod", [B, 2 * E]), sb("ex", [B, E]), sb("sc", [B, E])
        mx, sm, rs = sb("mx", [B, 1]), sb("sm", [B, 1]), sb("rs", [B, 1])
        g3, q3, low = sb("g3", [B, E, E]), sb("q3", [B, E, E]), sb("low", [B, E * E])
        rank, sel5 = sb("rank", [B, E]), sb("sel5", [B, E + 1])
        bs = sb("bs", [B, P])
        mtok, wtok = sb("mtok", [P, ROWS, E]), sb("wtok", [P, ROWS, E])
        eb2b = sb("eb2b", [P, E + 1, D])
        bank = [ctx.enter_context(nc.psum_tensor(f"bank{i}", [P, 512], F32)) for i in range(8)]

        in_w0, in_u0, in_small, in_late = sem("in_w0"), sem("in_u0"), sem("in_small"), sem("in_late")
        in_x = [sem(f"in_x{i}") for i in range(N_TILES)]
        staged = [sem(f"staged{i}") for i in range(N_STAGE)]
        stage_free = sem("stage_free")
        late_split = sem("late_split")
        out_done = sem("out_done")
        dve_step, pool_step, act_step = sem("dve_step"), sem("pool_step"), sem("act_step")
        w0_ready, u0_ready, x0_split = sem("w0_ready"), sem("u0_ready"), sem("x0_split")
        v_psum, v_ready, p0_psum, p0_free = (sem(n) for n in (
            "v_psum", "v_ready", "p0_psum", "p0_free"))
        r_psum, z_psum, hh_psum = sem("r_psum"), sem("z_psum"), sem("hh_psum")
        r_sig, z_sig, hh_tanh = sem("r_sig"), sem("z_sig"), sem("hh_tanh")
        rh_hi_ready, rh_32_ready, rh_lo_ready = sem("rh_hi_ready"), sem("rh_32_ready"), sem("rh_lo_ready")
        nah_ready, zh_ready = sem("nah_ready"), sem("zh_ready")
        h_hi_ready, h_32_ready, h_lo_ready = sem("h_hi_ready"), sem("h_32_ready"), sem("h_lo_ready")
        x1_added = sem("x1_added")
        x1_split, p1_psum, p1_free = sem("x1_split"), sem("p1_psum"), sem("p1_free")
        gates1, logs1, lc1, exps1, elc1 = (sem(n) for n in ("gates1", "logs1", "lc1", "exps1", "elc1"))
        norm1 = sem("norm1")
        x2_split, p2_psum, p2_hi, p2_free = sem("x2_split"), sem("p2_psum"), sem("p2_hi"), sem("p2_free")
        seeds_ready = sem("seeds_ready")
        g_psum, f_psum, o_psum = sem("g_psum"), sem("f_psum"), sem("o_psum")
        g_tanh, f_tanh, o_tanh, c_tanh = sem("g_tanh"), sem("f_tanh"), sem("o_tanh"), sem("c_tanh")
        de_ready, c_ready = sem("de_ready"), sem("c_ready")
        s_hi_ready, s_32_ready, s_lo_ready = sem("s_hi_ready"), sem("s_32_ready"), sem("s_lo_ready")
        x3_added, x3_hi, x3_split = sem("x3_added"), sem("x3_hi"), sem("x3_split")
        up_psum, gelu_ready, gh_ready, gl_ready, down_done = (sem(n) for n in (
            "up_psum", "gelu_ready", "gh_ready", "gl_ready", "down_done"))
        part_ready, silu_ready, agg_ready, gate_psum = (sem(n) for n in (
            "part_ready", "silu_ready", "agg_ready", "gate_psum"))
        sgc_ready, mx_ready, ex_ready, sel_ready, wsel_psum, w_ready, y_ready, out_ready = (sem(n) for n in (
            "sgc_ready", "mx_ready", "ex_ready", "sel_ready", "wsel_psum", "w_ready", "y_ready", "out_ready"))

        block = ctx.enter_context(nc.Block())

        flat = lambda t: t[:, :, :].rearrange("p a n -> p (a n)")
        pieces = []
        for src, hi, lo, n in ((w1, flat(W1h), flat(W1l), K * 3 * D), (wr, flat(Wrh), flat(Wrl), K * 3 * D),
                               (wk, flat(Wkh), flat(Wkl), K * 3 * D),
                               (ew1, flat(E1h), flat(E1l), (E + 1) * K * HID),
                               (ew2, flat(E2h), flat(E2l), (E + 1) * FC * D)):
            for a in range(0, n, STAGE):
                m = min(STAGE, n - a)
                pieces.append((src[:, a:a + m], hi[:, a:a + m], lo[:, a:a + m], m))
        stage_u0 = pre[:, 0:K * 3 * D]
        stage_w0 = pre[:, K * 3 * D:2 * K * 3 * D]
        stage_c0 = stage[:, :, :].rearrange("p s n -> p (s n)")[:, 0:K * 3 * D].rearrange("p (k n) -> p k n", k=K)

        def tile_parts(ap):
            return ap.rearrange("p t c -> p (t c)").rearrange("p (h k n) -> p h k n", h=2, k=K)

        def split_view(i, k, h):
            return XS_n[:, 2 * i:2 * i + 2, h, k, :]

        @block.sync
        def _(sp):
            sp.dma_start(stage_w0, w0).then_inc(in_w0, 16)
            for i in range(N_TILES):
                cols = slice(i * NT, (i + 1) * NT)
                sp.dma_start(X[:, :, cols], xT[:, :, cols]).then_inc(in_x[i], 16)
                if i == 0:
                    for dst, src in ((cond[:, :, :], condT), (b0s[:, :], b0), (I[:, :], ident)):
                        sp.dma_start(dst, src).then_inc(in_small, 16)
                    sp.dma_start(stage_c0, c0).then_inc(in_small, 16)
                    sp.dma_start(stage_u0, u0).then_inc(in_u0, 16)
            for dst, src in ((b1s[:, :], b1), (eb1s[:, :], eb1), (eb2b[:, :, :], eb2), (gws[:, :, :], gate_w),
                             (tws[:, :, :], time_w), (sbb[:, :], small_b), (low[:, :], lower), (bs[:, :], bsel),
                             (mtok[:, :, :], mask_tok)):
                sp.dma_start(dst, src).then_inc(in_late, 16)
            sp.wait_ge(v_psum, 1)
            for n, (src, _, _, m) in enumerate(pieces):
                if n >= N_STAGE:
                    sp.wait_ge(stage_free, n - N_STAGE + 1)
                sp.dma_start(stage[:, n % N_STAGE, 0:m], src).then_inc(staged[n % N_STAGE], 16)
            for r in range(ROWS):
                i, q = divmod(r, SUB)
                sp.wait_ge(out_ready, r + 1)
                sp.dma_start(out[:, r * (P // B):(r + 1) * (P // B), :].rearrange("b t d -> t b d"),
                             X[:, q, i * TC:(i + 1) * TC]).then_inc(out_done, 16)
            sp.wait_ge(out_done, 16 * ROWS)

        @block.gpsimd
        def _(pool):
            for n, (_, hi, lo, m) in enumerate(pieces):
                src = stage[:, n % N_STAGE, 0:m]
                pool.wait_ge(staged[n % N_STAGE], 16 * (n // N_STAGE + 1))
                nc.gpsimd.tensor_scalar(src, src, SPLIT_SCALE, 1.0, ALU.mult, ALU.mult).then_inc(pool_step, 1)
                pool.wait_ge(pool_step, 2 * n + 1)
                if n == WK_PIECE:
                    pool.wait_ge(p0_psum, N_TILES * 3 * K)
                nc.gpsimd.tensor_copy(hi, src).then_inc(pool_step, 1)
                pool.wait_ge(pool_step, 2 * n + 2)
                nc.gpsimd.tensor_tensor(lo, src, hi, ALU.subtract).then_inc(stage_free, 1)

            def chunk(t0, c):
                if not (isinstance(t0, int) and t0 == 0):
                    pool.wait_ge(o_psum, t0 + (CHUNK * (c + 1) - TS))
                nc.gpsimd.tensor_copy(SEEDS[:, c * CHUNK:(c + 1) * CHUNK, :],
                                      PRE[:, bass.ds(t0 + c * CHUNK, CHUNK), :]).then_inc(seeds_ready, CHUNK)

            def split_x3(t0):
                pool.wait_ge(x3_added, t0 + TS)
                hi, lo = (tile_parts(XS_T[:, bass.ds(t0, TS), :])[:, h] for h in range(2))
                x = X[:, :, bass.ds(t0 * B, TC)]
                nc.gpsimd.tensor_copy(hi, x).then_inc(x3_hi, TS)
                pool.wait_ge(x3_hi, t0 + TS)
                nc.gpsimd.tensor_tensor(lo, x, hi, ALU.subtract).then_inc(x3_split, TS)

            pool.wait_ge(p2_free, 3 * K)
            for c in range(TS // CHUNK):
                chunk(0, c)
            for c in range(TS // CHUNK):
                chunk(TS, c)
            pool.wait_ge(p2_free, N_TILES * 3 * K)
            split_x3(0)
            with pool.Fori(2 * TS, T - TS + 1, TS) as t0:
                for c in range(TS // CHUNK):
                    chunk(t0, c)
                split_x3(t0 - TS)
            split_x3(T - TS)

        flat3 = lambda t: t.rearrange("p a c -> p (a c)")

        def products(out_ap, wh, wl, i, m):
            cols = slice(m * P, (m + 1) * P)
            for k in range(K):
                for n, (w, h) in enumerate(((wh, 0), (wl, 0), (wh, 1))):
                    last = nc.tensor.matmul(out_ap.rearrange("p (a n) -> p a n", n=TC), w[:, k, cols],
                                            split_view(i, k, h), start=k == 0 and n == 0, stop=k == K - 1 and n == 2)
            return last

        def pairs(bank_):
            return bank_[:, 0:2 * K * B].rearrange("p (a c) -> p a c", c=2)

        def halves(t):
            return t.rearrange("p (k b) -> p k b", k=K)

        def gate_products(psum, wh, wl, a, gate, part, blocks=range(K)):
            for m in blocks:
                for k in range(K):
                    cols = slice((gate * K + m) * P, (gate * K + m + 1) * P)
                    for w in ((wh, wl) if part == "hi" else (wh,)):
                        last = nc.tensor.matmul(psum[:, m * B:(m + 1) * B], w[:, k, cols], a[:, k * B:(k + 1) * B],
                                                start=False, stop=part == "lo" and m == K - 1 and k == K - 1,
                                                skip_group_check=True)
            return last

        def seed(psum, src, gate):
            for h in range(2):
                at = (3 * h + gate) * K * B
                nc.tensor.matmul(psum[:, 0:K * B], I64[:, :], src[:, at:at + K * B], start=h == 0, stop=False,
                                 skip_group_check=True)

        def blocks_of(s):
            n = LAST_UP + 1
            return range(s * N_BLOCKS // n, (s + 1) * N_BLOCKS // n) if 0 <= s < n else range(0)

        @block.tensor
        def _(pe):
            pe.wait_ge(in_small, 64)
            for g in range(3 * K):
                for k in range(K):
                    last = nc.tensor.matmul(bank[7][:, g * B:(g + 1) * B], stage_c0[:, k, g * P:(g + 1) * P],
                                            cond[:, k, :], start=k == 0, stop=k == K - 1)
            last.then_inc(v_psum, 1)
            pe.wait_ge(w0_ready, 1)
            for i in range(N_TILES):
                pe.wait_ge(x0_split, i + 1)
                for g in range(3 * K):
                    n = i * 3 * K + g
                    if n >= 2:
                        pe.wait_ge(p0_free, n - 1)
                    products(bank[n % 2][:, :], W0h, W0l, i, g).then_inc(p0_psum, 1)
            R, Z, H = bank[2], bank[3], bank[4]
            pe.wait_ge(p0_free, N_TILES * 3 * K)
            pe.wait_ge(u0_ready, 1)
            with pe.Fori(0, T - UNROLL + 1, UNROLL) as t0:
                for u in range(UNROLL):
                    t = t0 + u
                    src = PRE[:, bass.ds(t, 1), :].rearrange("p t c -> p (t c)")
                    seed(R, src, 0)
                    seed(Z, src, 1)
                    pe.wait_ge(h_hi_ready, t + 1)
                    h16 = hs16[:, :, 1]
                    gate_products(R, U0h, U0l, h16, 0, "hi")
                    pe.wait_ge(h_lo_ready, t + 1)
                    gate_products(R, U0h, U0l, hl_, 0, "lo").then_inc(r_psum, 1)
                    gate_products(Z, U0h, U0l, h16, 1, "hi")
                    gate_products(Z, U0h, U0l, hl_, 1, "lo").then_inc(z_psum, 1)
                    seed(H, src, 2)
                    pe.wait_ge(rh_hi_ready, t + 1)
                    gate_products(H, U0h, U0l, rhh, 2, "hi")
                    pe.wait_ge(rh_lo_ready, t + 1)
                    gate_products(H, U0h, U0l, rhl, 2, "lo").then_inc(hh_psum, 1)
                    pe.wait_ge(z_sig, t + 1)
            pe.wait_ge(stage_free, 2)
            for i in range(N_TILES):
                pe.wait_ge(x1_split, i + 1)
                for g in range(3 * K):
                    n = i * 3 * K + g
                    if n >= 2:
                        pe.wait_ge(p1_free, n - 1)
                    products(bank[n % 2][:, :], W1h, W1l, i, g).then_inc(p1_psum, 1)
            def project2(n):
                i, g = divmod(n, 3 * K)
                if n >= 2:
                    pe.wait_ge(p2_free, n - 1)
                products(bank[n % 2][:, :], Wkh, Wkl, i, g).then_inc(p2_psum, 1)

            pe.wait_ge(stage_free, 6)
            for n in range(3 * K):
                if n == 0:
                    pe.wait_ge(x2_split, N_TILES)
                project2(n)

            Fb, Ob, Gb = bank[2], bank[3], bank[4]
            first = lambda t: isinstance(t, int) and t == 0

            def step2(t, s):
                if s % CHUNK == 0:
                    pe.wait_ge(seeds_ready, t + CHUNK)
                if not first(t):
                    pe.wait_ge(o_tanh, t)
                src = SEEDS[:, s, :]
                seed(Gb, src, 2)
                seed(Fb, src, 0)
                seed(Ob, src, 1)
                pe.wait_ge(s_hi_ready, t + 1)
                gate_products(Gb, Wrh, Wrl, hh_, 2, "hi")
                gate_products(Fb, Wrh, Wrl, hh_, 0, "hi", (0,))
                pe.wait_ge(s_lo_ready, t + 1)
                gate_products(Gb, Wrh, Wrl, hl_, 2, "lo").then_inc(g_psum, 1)
                gate_products(Fb, Wrh, Wrl, hh_, 0, "hi", (1,))
                gate_products(Fb, Wrh, Wrl, hl_, 0, "lo").then_inc(f_psum, 1)
                gate_products(Ob, Wrh, Wrl, hh_, 1, "hi")
                gate_products(Ob, Wrh, Wrl, hl_, 1, "lo").then_inc(o_psum, 1)

            def up(n, x):
                m, f = divmod(n, FC)
                for k in range(K):
                    cols = slice(k * HID + f * P, k * HID + (f + 1) * P)
                    for j, (w, h) in enumerate(((E1h, 0), (E1l, 0), (E1h, 1))):
                        last = nc.tensor.matmul(bank[n % 2][:, 0:TC], w[:, m, cols], x[:, h, k, :],
                                                start=k == 0 and j == 0, stop=k == K - 1 and j == 2)
                return last

            def down(n, x):
                m, f = divmod(n, FC)
                acc = bank[5 + m % 2]
                for q in range(SUB):
                    rows = acc[:, q * D:(q + 1) * D]
                    for j, (part, w) in enumerate(((Gh, E2h), (Gh, E2l), (Gl, E2h))):
                        last = nc.tensor.matmul(rows, part[:, n % 4, q * P:(q + 1) * P], w[:, m, f * D:(f + 1) * D],
                                                start=f == 0 and q == 0 and j == 0, stop=False, skip_group_check=True)
                    if n == 0:
                        for k in range(K):
                            for h in range(2):
                                last = nc.tensor.matmul(acc[:, q * D + k * P:q * D + (k + 1) * P],
                                                        x[:, h, k, q * P:(q + 1) * P], I64[:, :],
                                                        start=False, stop=False, skip_group_check=True)
                return last

            def routing_products():
                pe.wait_ge(in_late, IN_LATE)
                pe.wait_ge(silu_ready, 1)
                for k in range(K):
                    nc.tensor.matmul(bank[2][0:B, 0:2 * E], silu[:, k, :], tws[:, k, :], start=k == 0, stop=k == K - 1)
                pe.wait_ge(agg_ready, 1)
                for a in range(3):
                    for k in range(K):
                        last = nc.tensor.matmul(bank[3][0:B, 0:E], agg[:, a, k * B:(k + 1) * B], gws[:, a * K + k, :],
                                                start=a == 0 and k == 0, stop=a == 2 and k == K - 1)
                last.then_inc(gate_psum, 1)

            n_after = (N_TILES - 1) * 3 * K
            for s in range(TS):
                step2(s, s)
                for n in range(s * n_after // TS, (s + 1) * n_after // TS):
                    project2(3 * K + n)
            pe.wait_ge(stage_free, len(pieces))
            with pe.Fori(TS, T - TS + 1, TS) as t0:
                x = tile_parts(XS_T[:, bass.ds(t0 - TS, TS), :])
                for s in range(TS):
                    t = t0 + s
                    step2(t, s)
                    if s == 0:
                        pe.wait_ge(x3_split, t)
                    if blocks_of(s):
                        pe.wait_ge(gelu_ready, t)
                        for n in blocks_of(s):
                            last = up(n, x)
                        last.then_inc(up_psum, 2 if s == LAST_UP else 1)
                    if blocks_of(s - 1):
                        pe.wait_ge(gl_ready, t)
                        for n in blocks_of(s - 1):
                            last = down(n, x)
                        last.then_inc(down_done, 2 if s == 1 else 1)
            x = tile_parts(XS_T[:, T - TS:T, :])
            pe.wait_ge(x3_split, T)
            for n in range(N_BLOCKS + 2):
                if n < N_BLOCKS:
                    pe.wait_ge(gelu_ready, T + max(n - 1, 0))
                    up(n, x).then_inc(up_psum, 1)
                if n == 1:
                    routing_products()
                if n == ROUTED:
                    pe.wait_ge(sel_ready, 1)
                    nc.tensor.matmul(bank[4][:, 0:E], bs[:, :], sel5[:, 0:E], start=True, stop=True).then_inc(wsel_psum, 1)
                if n >= 2:
                    pe.wait_ge(gl_ready, T + n - 1)
                    down(n - 2, x).then_inc(down_done, 1)

        def tile_view(ap):
            return ap.rearrange("p (t b) -> p t b", b=B)

        @block.scalar
        def _(act):
            nc.scalar.preload_act_table(ACT.Sigmoid)
            with act.Fori(0, T - UNROLL + 1, UNROLL) as t0:
                for u in range(UNROLL):
                    t = t0 + u
                    act.wait_ge(r_psum, t + 1)
                    nc.scalar.activation(gr[:, :], bank[2][:, 0:K * B], ACT.Sigmoid, scale=UNSCALE).then_inc(r_sig, 1)
                    act.wait_ge(z_psum, t + 1)
                    nc.scalar.activation(fma_m[:, :, 1], bank[3][:, 0:K * B], ACT.Sigmoid, scale=UNSCALE).then_inc(z_sig, 1)
                    act.wait_ge(hh_psum, t + 1)
                    nc.scalar.activation(fma_ab[:, :, 0], bank[4][:, 0:K * B], ACT.Tanh, scale=UNSCALE).then_inc(hh_tanh, 1)
            act.wait_ge(in_late, IN_LATE)
            for i in range(N_TILES):
                for g in range(3 * K):
                    n = i * 3 * K + g
                    act.wait_ge(p1_psum, n + 1)
                    dst = (bufA, bufB, bufC)[g // K][:, g % K, i * NT:(i + 1) * NT]
                    nc.scalar.activation(dst, bank[n % 2][:, :], ACT.Sigmoid if g < 2 * K else ACT.Identity,
                                         bias=b1s[:, g:g + 1], scale=UNSCALE).then_inc(p1_free, 1)
            nc.scalar.activation(sgc[:, :, :], cond[:, :, :], ACT.Sigmoid).then_inc(sgc_ready, 1)
            act.wait_ge(norm1, 1)
            nc.scalar.activation(bufA[:, :, :], bufA[:, :, :], ACT.Ln, bias=eps[:, 0:1]).then_inc(logs1, 1)
            act.wait_ge(lc1, K * B)
            nc.scalar.activation(bufA[:, :, 0:B], bufC[:, :, TOK - B:TOK], ACT.Exp).then_inc(exps1, 1)
            for k in range(K):
                for b in range(B):
                    nc.scalar.activation(tile_view(bufA[:, k, :])[:, 1:T, b], tile_view(bufC[:, k, :])[:, 0:T - 1, b],
                                         ACT.Exp, bias=bufC[:, k, TOK - B + b:TOK - B + b + 1], scale=-1.0)\
                        .then_inc(exps1, 1)
            nc.scalar.activation(bufD[:, :, :], bufC[:, :, :], ACT.Exp).then_inc(elc1, 1)
            def pre2_high(n):
                i, g = divmod(n, 3 * K)
                act.wait_ge(p2_psum, n + 1)
                nc.scalar.activation(PRE[:, i * TT:(i + 1) * TT, g * B:(g + 1) * B], tile_view(bank[n % 2][:, :]),
                                     ACT.Identity, scale=2 * UNSCALE).then_inc(p2_hi, 1)

            nc.scalar.preload_act_table(ACT.Gelu_apprx_tanh)
            for n in range(3 * K):
                pre2_high(n)

            def step2(t):
                act.wait_ge(g_psum, t + 1)
                nc.scalar.activation(gh[:, :], bank[4][:, 0:K * B], ACT.Tanh, scale=UNSCALE / 2).then_inc(g_tanh, 1)
                act.wait_ge(f_psum, t + 1)
                nc.scalar.activation(fma_m[:, :, 1], bank[2][:, 0:K * B], ACT.Tanh, scale=UNSCALE / 4)\
                    .then_inc(f_tanh, 1)
                act.wait_ge(o_psum, t + 1)
                nc.scalar.activation(gz[:, :], bank[3][:, 0:K * B], ACT.Tanh, scale=UNSCALE / 4).then_inc(o_tanh, 1)
                act.wait_ge(c_ready, t + 2)
                nc.scalar.activation(tcell[:, :], pairs(bank[7])[:, :, 1], ACT.Tanh, scale=0.5).then_inc(c_tanh, 1)

            def gelu(n):
                return nc.scalar.activation(G[:, n % 2, :], bank[n % 2][:, 0:TC], ACT.Gelu_apprx_tanh,
                                            bias=eb1s[:, n:n + 1], scale=UNSCALE)

            n_after = (N_TILES - 1) * 3 * K
            for s in range(TS):
                step2(s)
                for n in range(s * n_after // TS, (s + 1) * n_after // TS):
                    pre2_high(3 * K + n)
            with act.Fori(TS, T - TS + 1, TS) as t0:
                for s in range(TS):
                    t = t0 + s
                    step2(t)
                    if blocks_of(s):
                        act.wait_ge(up_psum, t + 1)
                        act.wait_ge(gl_ready, t)
                        for n in blocks_of(s):
                            last = gelu(n)
                        last.then_inc(gelu_ready, 2 if s == LAST_UP else 1)
            for n in range(N_BLOCKS):
                if n == 2:
                    act.wait_ge(mx_ready, 1)
                    nc.scalar.activation(ex[:, :], lg[:, :], ACT.Exp, bias=mx[:, 0:1]).then_inc(ex_ready, 1)
                    nc.scalar.preload_act_table(ACT.Gelu_apprx_tanh)
                act.wait_ge(up_psum, T + n + 1)
                act.wait_ge(gl_ready, T + max(n - 1, 0))
                gelu(n).then_inc(gelu_ready, 1)

        @block.vector
        def _(dve):
            steps = [0]

            def then_wait(ins):
                steps[0] += 1
                ins.then_inc(dve_step, 1)
                dve.wait_ge(dve_step, steps[0])

            def split_weights(src, hi, lo, done):
                then_wait(nc.vector.tensor_scalar(hi, src, SPLIT_SCALE, None, ALU.mult))
                nc.vector.scalar_tensor_tensor(lo, src, SPLIT_SCALE, hi, ALU.mult, ALU.subtract).then_inc(done, 1)

            def split_x(i, done):
                src = X[:, :, i * NT:(i + 1) * NT].rearrange("p k (a n) -> p a k n", n=TC)
                hi, lo = (XS_n[:, 2 * i:2 * i + 2, h] for h in range(2))
                for a in range(2):
                    ins = nc.vector.tensor_copy(hi[:, a], src[:, a])
                then_wait(ins)
                for a in range(2):
                    ins = nc.vector.tensor_tensor(lo[:, a], src[:, a], hi[:, a], ALU.subtract)
                ins.then_inc(done, 1)

            nc.vector.memset(zeros[:, :], 0.0)
            nc.vector.memset(eps[:, :], EPS).then_inc(dve_step, 1)
            steps[0] += 1
            for n, begun in enumerate((up_psum, gelu_ready, gh_ready, gl_ready, down_done)):
                nc.vector.memset(mark[:, n:n + 1], 0.0).then_inc(begun, TS)
            nc.vector.memset(fma_m[:, :, :], 0.0)
            nc.vector.memset(hs32[:, :, :, :], 0.0).then_inc(h_32_ready, 1)
            nc.vector.memset(hs16[:, :, :], 0.0).then_inc(h_hi_ready, 1)
            nc.vector.memset(hl_[:, :], 0.0).then_inc(h_lo_ready, 1)
            dve.wait_ge(in_w0, 16)
            split_weights(stage_w0, flat(W0h), flat(W0l), w0_ready)
            for i in range(N_TILES):
                dve.wait_ge(in_x[i], 16)
                split_x(i, x0_split)
                if i == 0:
                    dve.wait_ge(in_u0, 16)
                    split_weights(stage_u0, flat(U0h), flat(U0l), u0_ready)
            dve.wait_ge(in_small, 64)
            nc.vector.tensor_scalar(I64[:, :], I[:, :], SPLIT_SCALE, None, ALU.mult).then_inc(v_ready, 1)
            dve.wait_ge(v_psum, 1)
            then_wait(nc.vector.tensor_tensor(v0[:, :, :], bank[7][:, 0:3 * K * B].rearrange("p (g b) -> p g b", b=B),
                                              b0s[:, :, None].broadcast_to([P, 3 * K, B]), ALU.add))
            dve.wait_ge(u0_ready, 1)
            for n in range(N_TILES * 3 * K):
                i, g = divmod(n, 3 * K)
                hi, lo = (PRE[:, i * TT:(i + 1) * TT, (3 * K * h + g) * B:(3 * K * h + g + 1) * B] for h in range(2))
                v = v0[:, g:g + 1, :].broadcast_to([P, TT, B])
                dve.wait_ge(p0_psum, n + 1)
                nc.vector.scalar_tensor_tensor(hi, tile_view(bank[n % 2][:, :]), UNSCALE, v, ALU.mult, ALU.add)
                if n:
                    dve.wait_ge(p0_free, n)
                then_wait(nc.vector.scalar_tensor_tensor(tile_view(preproj[:, :]), tile_view(bank[n % 2][:, :]),
                                                         UNSCALE, v, ALU.mult, ALU.add))
                nc.vector.tensor_tensor(lo, tile_view(preproj[:, :]), hi, ALU.subtract).then_inc(p0_free, 1)

            def fma(out_):
                return nc.vector.tensor_tensor_scan(out_, flat3(fma_m[:, :, :]), flat3(fma_ab[:, :, :]), 0.0,
                                                    ALU.mult, ALU.add)

            with dve.Fori(0, T - UNROLL + 1, UNROLL) as t0:
                for u in range(UNROLL):
                    t = t0 + u
                    h, new = hs32[:, u % 2, :, 1], hs32[:, (u + 1) % 2]
                    dve.wait_ge(r_sig, t + 1)
                    nc.vector.tensor_tensor(rhh[:, :], gr[:, :], h, ALU.mult).then_inc(rh_hi_ready, 1)
                    nc.vector.tensor_tensor(rh32[:, :], gr[:, :], h, ALU.mult).then_inc(rh_32_ready, 1)
                    dve.wait_ge(rh_32_ready, t + 1)
                    nc.vector.tensor_tensor(rhl[:, :], rh32[:, :], rhh[:, :], ALU.subtract).then_inc(rh_lo_ready, 1)
                    dve.wait_ge(z_sig, t + 1)
                    nc.vector.scalar_tensor_tensor(fma_ab[:, :, 1], fma_m[:, :, 1], 1.0, h, ALU.subtract, ALU.mult,
                                                   reverse0=True).then_inc(zh_ready, 1)
                    dve.wait_ge(hh_tanh, t + 1)
                    dve.wait_ge(zh_ready, t + 1)
                    fma(flat3(hs16[:, :, :])).then_inc(h_hi_ready, 1)
                    fma(flat3(new)).then_inc(h_32_ready, 1)
                    dve.wait_ge(h_32_ready, t + 2)
                    nc.vector.tensor_tensor(hl_[:, :], new[:, :, 1], hs16[:, :, 1], ALU.subtract).then_inc(h_lo_ready, 1)
                    xs = X[:, :, bass.ds(t * B, B)]
                    nc.vector.tensor_tensor(xs, xs, new[:, :, 1].rearrange("p (k b) -> p k b", k=K), ALU.add).then_inc(x1_added, 1)

            dve.wait_ge(x1_added, T)
            for i in range(N_TILES):
                split_x(i, x1_split)
            dve.wait_ge(p1_free, N_TILES * 3 * K)
            A_, B_, C_, D_ = (x[:, :, :] for x in (bufA, bufB, bufC, bufD))
            then_wait(nc.vector.scalar_tensor_tensor(D_, A_, EPS, B_, ALU.add, ALU.add))
            then_wait(nc.vector.reciprocal(D_, D_))
            nc.vector.tensor_tensor(A_, A_, D_, ALU.mult).then_inc(norm1, 1)
            then_wait(nc.vector.tensor_tensor(B_, B_, D_, ALU.mult))
            then_wait(nc.vector.tensor_tensor(B_, B_, C_, ALU.mult))

            def cumsum(dst, src, done):
                for k in range(K):
                    for b in range(B):
                        nc.vector.tensor_tensor_scan(tile_view(dst[:, k, :])[:, :, b], tile_view(src[:, k, :])[:, :, b],
                                                     zeros[:, :], 0.0, ALU.add, ALU.add).then_inc(done, 1)

            dve.wait_ge(logs1, 1)
            cumsum(bufC, bufA, lc1)
            dve.wait_ge(exps1, 1 + K * B)
            then_wait(nc.vector.tensor_tensor(B_, B_, A_, ALU.mult))
            cumsum(bufA, bufB, lc1)
            dve.wait_ge(elc1, 1)
            for k in range(K):
                d = tile_view(bufD[:, k, :])
                ins = nc.vector.tensor_tensor(d, d, cond[:, k:k + 1, :].broadcast_to([P, T, B]), ALU.mult)
            dve.wait_ge(lc1, 2 * K * B)
            then_wait(ins)
            then_wait(nc.vector.tensor_tensor(A_, A_, D_, ALU.add))
            then_wait(nc.vector.tensor_tensor(X[:, :, :], X[:, :, :], A_, ALU.add))

            for i in range(N_TILES):
                split_x(i, x2_split)
            dve.wait_ge(sgc_ready, 1)
            nc.vector.tensor_tensor(silu[:, :, :], sgc[:, :, :], cond[:, :, :], ALU.mult).then_inc(silu_ready, 1)

            def pre2_low(n):
                i, g = divmod(n, 3 * K)
                hi, lo = (PRE[:, i * TT:(i + 1) * TT, (3 * K * h + g) * B:(3 * K * h + g + 1) * B] for h in range(2))
                dve.wait_ge(p2_hi, n + 1)
                nc.vector.scalar_tensor_tensor(lo, tile_view(bank[n % 2][:, :]), 2 * UNSCALE, hi, ALU.mult, ALU.subtract)\
                    .then_inc(p2_free, 1)

            cell = pairs(bank[7])[:, :, 1]
            nc.vector.tensor_scalar(halves(cell), cond[:, :, :], 2.0, None, ALU.mult).then_inc(c_ready, 1)
            nc.vector.tensor_scalar(halves(hh_[:, :]), cond[:, :, :], 2.0, None, ALU.mult).then_inc(s_hi_ready, 1)
            dve.wait_ge(s_hi_ready, 1)
            nc.vector.scalar_tensor_tensor(halves(hl_[:, :]), cond[:, :, :], 2.0, halves(hh_[:, :]),
                                           ALU.mult, ALU.subtract).then_inc(s_lo_ready, 1)
            for n in range(3 * K):
                pre2_low(n)

            def step2(t, s):
                dve.wait_ge(g_tanh, t + 1)
                if s == 0:
                    dve.wait_ge(c_ready, t + 1)
                nc.vector.scalar_tensor_tensor(fma_ab[:, :, 0], cell, 0.5, gh[:, :], ALU.mult, ALU.subtract)
                nc.vector.scalar_tensor_tensor(fma_ab[:, :, 1], cell, 0.5, gh[:, :], ALU.mult, ALU.add)\
                    .then_inc(de_ready, 1)
                dve.wait_ge(f_tanh, t + 1)
                dve.wait_ge(de_ready, t + 1)
                fma(bank[7][:, 0:2 * K * B]).then_inc(c_ready, 1)
                dve.wait_ge(c_tanh, t + 1)
                nc.vector.scalar_tensor_tensor(hh_[:, :], gz[:, :], 1.0, tcell[:, :], ALU.add, ALU.mult)\
                    .then_inc(s_hi_ready, 1)
                h = h32[:, s % 2, :]
                nc.vector.scalar_tensor_tensor(h, gz[:, :], 1.0, tcell[:, :], ALU.add, ALU.mult)\
                    .then_inc(s_32_ready, 1)
                dve.wait_ge(s_32_ready, t + 1)
                nc.vector.tensor_tensor(hl_[:, :], h, hh_[:, :], ALU.subtract).then_inc(s_lo_ready, 1)
                xs = X[:, :, bass.ds(t * B, B)]
                nc.vector.scalar_tensor_tensor(xs, halves(h), 0.5, xs, ALU.mult, ALU.add).then_inc(x3_added, 1)

            def split_gelus(blocks, count, done, used):
                dve.wait_ge(gelu_ready, count)
                dve.wait_ge(down_done, used)
                for n in blocks:
                    last = nc.vector.tensor_copy(Gh[:, n % 4, :], G[:, n % 2, :])
                last.then_inc(gh_ready, done)
                dve.wait_ge(gh_ready, count + (done - 1))
                for n in blocks:
                    last = nc.vector.tensor_tensor(Gl[:, n % 4, :], G[:, n % 2, :], Gh[:, n % 4, :], ALU.subtract)
                last.then_inc(gl_ready, done)

            def network_rows(m, t0, count):
                dve.wait_ge(down_done, count)
                if m == 0:
                    dst = X[:, :, bass.ds(t0 * B, TC)]
                elif m < E:
                    dst = flat3(PRE_Y[:, bass.ds(t0, TS), :])[:, (m - 1) * SUB * D:m * SUB * D]
                else:
                    dst = flat3(XS_Y[:, bass.ds(t0, TS), :])
                if m:
                    dst = dst.rearrange("p (q n) -> p q n", q=SUB)
                nc.vector.scalar_tensor_tensor(dst, bank[5 + m % 2][:, :].rearrange("p (q n) -> p q n", q=SUB), UNSCALE,
                                               eb2b[:, m:m + 1, :].broadcast_to([P, SUB, D]), ALU.mult, ALU.add)\
                    .then_inc(y_ready, 1)

            def stretch_sums(t0):
                x = X[:, :, bass.ds(t0 * B, TC)].rearrange("p k (t b) -> p k b t", b=B)
                sums = flat3(part[:, bass.ds(t0, TS), :])
                for i, (a, z) in enumerate(zip(CUTS, CUTS[1:])):
                    nc.vector.tensor_reduce(halves(sums[:, i * K * B:(i + 1) * K * B]), x[:, :, :, a:z], AX_X, ALU.add)\
                        .then_inc(part_ready, 1)

            n_after = (N_TILES - 1) * 3 * K
            for s in range(TS):
                step2(s, s)
                for n in range(s * n_after // TS, (s + 1) * n_after // TS):
                    pre2_low(3 * K + n)
            dve.wait_ge(in_late, IN_LATE)
            with dve.Fori(TS, T - TS + 1, TS) as t0:
                for s in range(TS):
                    t = t0 + s
                    step2(t, s)
                    if s == 0:
                        stretch_sums(t0 - TS)
                    if blocks_of(s):
                        split_gelus(blocks_of(s), t + 1, 2 if s == LAST_UP else 1, t)
                    for n in blocks_of(s - 1):
                        if n % FC == FC - 1:
                            network_rows(n // FC, t0 - TS, t + 1)

            dve.wait_ge(x3_added, T)
            stretch_sums(T - TS)
            dve.wait_ge(part_ready, 3 * N_TILES3)
            sums = part[:, :, :].rearrange("p (i t) c -> p i (t c)", t=TS)
            ends = (0, L_HEAD, 2 * L_HEAD, T)
            for g in range(3):
                for i, (a, z) in enumerate(zip(CUTS, CUTS[1:])):
                    tiles = [j for j in range(N_TILES3) if ends[g] <= j * TS + a and j * TS + z <= ends[g + 1]]
                    ins = nc.vector.tensor_reduce(part9[:, g, i, :],
                                                  sums[:, tiles[0]:tiles[-1] + 1, i * K * B:(i + 1) * K * B]
                                                  .rearrange("p i c -> p c i"), AX_X, ALU.add)
            then_wait(ins)
            then_wait(nc.vector.tensor_reduce(seg[:, :, :], part9[:, :, :, :].rearrange("p g i c -> p g c i"),
                                              AX_X, ALU.add))
            nc.vector.tensor_tensor(agg[:, 1, :], seg[:, 0, :], seg[:, 2, :], ALU.add)
            then_wait(nc.vector.tensor_tensor(agg[:, 2, :], seg[:, 1, :], seg[:, 2, :], ALU.add))
            then_wait(nc.vector.tensor_tensor(agg[:, 0, :], agg[:, 1, :], seg[:, 1, :], ALU.add))
            nc.vector.tensor_scalar(agg[:, 0, :], agg[:, 0, :], 1.0 / T, None, ALU.mult)
            nc.vector.tensor_scalar(agg[:, 1:3, :], agg[:, 1:3, :], 1.0 / (L_HEAD + L_PROPRIO), None, ALU.mult)\
                .then_inc(agg_ready, 1)
            dve.wait_ge(gate_psum, 1)
            then_wait(nc.vector.tensor_tensor(mod[:, :], bank[2][0:B, 0:2 * E], sbb[:, E:3 * E], ALU.add))
            then_wait(nc.vector.tensor_tensor(lg[:, :], bank[3][0:B, 0:E], sbb[:, 0:E], ALU.add))
            then_wait(nc.vector.scalar_tensor_tensor(lg[:, :], mod[:, 0:E], 1.0, lg[:, :], ALU.add, ALU.mult))
            then_wait(nc.vector.tensor_tensor(lg[:, :], lg[:, :], mod[:, E:2 * E], ALU.add))
            then_wait(nc.vector.reduce_max(mx[:, :], lg[:, :], AX_X))
            nc.vector.tensor_scalar(mx[:, :], mx[:, :], -1.0, None, ALU.mult).then_inc(mx_ready, 1)

            def tail_block(n):
                split_gelus((n,), T + n + 1, 1, T + max(n - 3, 0))

            for n in range(2):
                tail_block(n)
            dve.wait_ge(ex_ready, 1)
            then_wait(nc.vector.reduce_sum(sm[:, :], ex[:, :], AX_X))
            then_wait(nc.vector.reciprocal(rs[:, :], sm[:, :]))
            then_wait(nc.vector.tensor_scalar(sc[:, :], ex[:, :], rs[:, 0:1], None, ALU.mult))
            scj = sc[:, None, :].broadcast_to([B, E, E])
            sce = sc[:, :, None].broadcast_to([B, E, E])
            then_wait(nc.vector.tensor_tensor(g3[:, :, :], scj, sce, ALU.is_gt))
            then_wait(nc.vector.tensor_tensor(q3[:, :, :], scj, sce, ALU.is_equal))
            then_wait(nc.vector.tensor_tensor(q3[:, :, :], q3[:, :, :], low[:, :].rearrange("p (e j) -> p e j", e=E), ALU.mult))
            then_wait(nc.vector.tensor_tensor(g3[:, :, :], g3[:, :, :], q3[:, :, :], ALU.add))
            then_wait(nc.vector.reduce_sum(rank[:, :], g3[:, :, :], AX_X))
            then_wait(nc.vector.scalar_tensor_tensor(sel5[:, 0:E], rank[:, :], 1.5, sc[:, :], ALU.is_lt, ALU.mult))
            then_wait(nc.vector.reduce_sum(sm[:, :], sel5[:, 0:E], AX_X))
            then_wait(nc.vector.tensor_scalar(sm[:, :], sm[:, :], EPS, None, ALU.add))
            then_wait(nc.vector.reciprocal(rs[:, :], sm[:, :]))
            then_wait(nc.vector.tensor_scalar(sel5[:, 0:E], sel5[:, 0:E], rs[:, 0:1], None, ALU.mult))
            nc.vector.memset(sel5[:, E:E + 1], 1.0).then_inc(sel_ready, 1)

            def add_routed(r):
                i, q = divmod(r, SUB)
                row = X[:, q, i * TC:(i + 1) * TC]
                for e in range(E):
                    if e < E - 1:
                        y = flat3(PRE_Y[:, i * TS:(i + 1) * TS, :])[:, (e * SUB + q) * D:(e * SUB + q + 1) * D]
                    else:
                        y = flat3(XS_Y[:, i * TS:(i + 1) * TS, :])[:, q * D:(q + 1) * D]
                    ins = nc.vector.scalar_tensor_tensor(row, y, wtok[:, r, e:e + 1], row, ALU.mult, ALU.add)
                    if e < E - 1:
                        then_wait(ins)
                ins.then_inc(out_ready, 1)

            done_rows = ROWS - SUB
            for n in range(2, N_BLOCKS):
                tail_block(n)
                if n == ROUTED:
                    dve.wait_ge(wsel_psum, 1)
                    then_wait(nc.vector.tensor_tensor(wtok[:, :, :], bank[4][:, None, 0:E].broadcast_to([P, ROWS, E]),
                                                      mtok[:, :, :], ALU.mult))
                    dve.wait_ge(y_ready, (E + 1) * (N_TILES3 - 1))
                if n >= FC + 2 and (n - 2) % FC == 0:
                    network_rows((n - 2) // FC - 1, T - TS, T + n - 2)
                if n > ROUTED:
                    slots = N_BLOCKS - ROUTED - 1
                    k = n - ROUTED - 1
                    for r in range(k * done_rows // slots, (k + 1) * done_rows // slots):
                        add_routed(r)
            network_rows(E, T - TS, T + N_BLOCKS)
            dve.wait_ge(y_ready, (E + 1) * N_TILES3)
            for r in range(done_rows, ROWS):
                add_routed(r)


def kernel(**inputs):
    import numpy as np
    import concourse.bacc as bacc
    from concourse.bass_utils import run_bass_kernel_spmd as run

    g = {n: np.asarray(a) for n, a in inputs.items()}

    def halves_first(w):
        return w.reshape(K, P, -1).transpose(1, 0, 2)

    def columns(*bs):
        return np.concatenate(bs).reshape(-1, P).T

    def gates(*ws):
        return halves_first(np.concatenate(ws, axis=1)).reshape(P, -1)

    c = lambda n: g["L0_cond_" + n]
    f = lambda n: g["L1_cond_" + n]
    m = lambda n: g["L3_cond_" + n]
    t = np.arange(T)
    mask = np.ones((E, T), np.float32)
    mask[1, L_HEAD:2 * L_HEAD] = 0.0
    mask[2, :L_HEAD] = 0.0
    by_row = mask.reshape(E, ROWS, P // B, 1).repeat(B, axis=3).reshape(E, ROWS, P)
    arrays = {
        "xT": g["x"].transpose(2, 1, 0).reshape(K, P, TOK).transpose(1, 0, 2),
        "condT": halves_first(g["cond_1024"].T),
        "w0": gates(c("W_r"), c("W_z"), c("W")),
        "u0": gates(c("U_r"), c("U_z"), c("U")),
        "c0": gates(c("C_r"), c("C_z"), c("C")).reshape(P, K, 3 * D),
        "b0": columns(c("b_r"), c("b_z"), c("b")),
        "w1": gates(f("W_f").T, f("W_i").T, f("W_h").T),
        "b1": columns(f("b_f"), f("b_i"), f("b_h")),
        "wk": gates(g["L2_cond_Wk"]),
        "wr": gates(g["L2_cond_Wr"]),
        "gate_w": m("gate_w").reshape(3 * K, P, E).transpose(1, 0, 2),
        "time_w": halves_first(m("time_w")),
        "small_b": np.broadcast_to(np.concatenate([m("gate_b"), m("time_b")]), (B, 3 * E)),
        "eb1": columns(m("sb1"), m("eb1").ravel()),
        "eb2": np.broadcast_to(np.concatenate([m("sb2")[None], m("eb2")]), (P, E + 1, D)),
        "ew1": np.concatenate([m("sw1")[None], m("ew1")]).reshape(E + 1, K, P, HID).transpose(2, 0, 1, 3).reshape(P, -1),
        "ew2": np.concatenate([m("sw2")[None], m("ew2")]).reshape(E + 1, FC, P, D).transpose(2, 0, 1, 3).reshape(P, -1),
        "ident": np.eye(P, dtype=np.float32),
        "bsel": (np.arange(P)[None] % B == np.arange(B)[:, None]).astype(np.float32),
        "lower": np.broadcast_to(np.tril(np.ones((E, E), np.float32), -1).reshape(1, E * E), (B, E * E)),
        "mask_tok": by_row.transpose(2, 1, 0),
    }
    nc = bacc.Bacc("TRN2", target_bir_lowering=False, num_devices=1)
    arrays = {n: np.ascontiguousarray(a) for n, a in arrays.items()}
    aps = {n: nc.dram_tensor("in_" + n, a.shape, mybir.dt.from_np(a.dtype), kind="ExternalInput").ap()
           for n, a in arrays.items()}
    out = nc.dram_tensor("out_0", (B, T, D), F32, kind="ExternalOutput").ap()
    build(nc, **aps, out=out)
    r = run(nc, [{"in_" + n: a for n, a in arrays.items()}], core_ids=[0])
    return r.results[0]["out_0"]
```

```python
from contextlib import ExitStack

import concourse.bass as bass
from concourse import mybir

F32 = mybir.dt.float32
F16 = mybir.dt.float16
ACT = mybir.ActivationFunctionType
ALU = mybir.AluOpType
AX_X = mybir.AxisListType.X

P = 128
B, T, D = 8, 256, 256
K = D // P
TOK = B * T
SPLIT_SCALE = 64.0
UNSCALE = 1.0 / SPLIT_SCALE
EPS = 1e-8
E = 4
HID = 1024
FC = HID // P
TS = 16
TC = TS * B
N_TILES = T // TS
LAST_UP = TS - 2
MAX_BLOCKS = -(-(E + 1) * FC // (LAST_UP + 1))
CH = 8
CC = CH * B
PAIR = 2 * CH
NT = 512
N_LOADS = TOK // NT
L_HEAD = T // 3
L_PROPRIO = T - 2 * L_HEAD
CUTS = [0, *sorted((L_HEAD % TS, 2 * L_HEAD % TS)), TS]
HEAD, WRIST = range(0, L_HEAD // TS), range(-(-L_HEAD // TS), 2 * L_HEAD // TS)


def networks(tile):
    masked = [1 + 2] if tile in HEAD else [1 + 1] if tile in WRIST else []
    return [m for m in range(E + 1) if m not in masked]


STAGE = 1024
N_STAGE = 2
BY_POOL = (1, 3, 6, 8, 11, 13)
ROUTED = 4
IN_LATE = 16 * 9
DOUBLED = K * D


def build(nc, xT, condT, w0, u0, c0, b0, w1, b1, wk, wr, gate_w, time_w, small_b, eb1, eb2,
          ew1, ew2, ident, bsel, lower, mask_tok, out):
    with ExitStack() as ctx:
        def sb(name, shape, dt=F32):
            return ctx.enter_context(nc.sbuf_tensor(name, shape, dt))

        def sem(name):
            return ctx.enter_context(nc.semaphore(name))

        X = sb("X", [P, K, TOK])
        pre = sb("pre", [P, 3 * K * TOK])
        bufG, bufI = (pre[:, i * K * TOK:(i + 1) * K * TOK].rearrange("p (j t) -> p j t", t=T) for i in range(2))
        temps = [2 * K * TOK]

        def temp(n):
            temps[0] += n
            return pre[:, temps[0] - n:temps[0]]

        f_c, i_c, c_c, sum_c, norm_f, norm_i = (temp(K * CC).rearrange("p (k n) -> p k n", k=K) for _ in range(6))
        decay_m, decay_a, decay = (temp(K * B * (CH + 1)).rearrange("p (j t) -> p j t", t=CH + 1) for _ in range(3))
        I = temp(P)
        x1_parts = temp(K * CC).bitcast(F16).rearrange("p (h k n) -> p h k n", h=2, k=K)
        rows_y = pre[:, :].rearrange("p (t c) -> p t c", c=3 * K * B)
        rows_last = sb("rows_last", [P, T, K * B])
        x_parts = sb("x_parts", [P, 2, 2, K, CC], F16)
        x_double = sb("x_double", [P, K, CC])
        stage = sb("stage", [P, N_STAGE, STAGE])
        flat_stage = stage[:, :, :].rearrange("p s n -> p (s n)")
        gate_weights = lambda name: (sb(name + "h", [P, 3, K, D], F16), sb(name + "l", [P, 3, K, D], F16))
        W0h, W0l = gate_weights("W0")
        G = flat_stage[:, 0:2 * MAX_BLOCKS * TC].rearrange("p (c j n) -> p c j n", c=2, n=TC)
        Gh, Gl = (flat_stage[:, a * MAX_BLOCKS * TC:(a + 1) * MAX_BLOCKS * TC].bitcast(F16)
                  .rearrange("p (c j n) -> p c j n", c=2, n=TC) for a in (2, 3))
        x3_parts = flat_stage[:, 4 * MAX_BLOCKS * TC:4 * MAX_BLOCKS * TC + 2 * K * TC].bitcast(F16)\
            .rearrange("p (i h k n) -> p i h k n", i=2, h=2, k=K)
        U0h, U0l = gate_weights("U0")
        W1h, W1l = gate_weights("W1")
        Wkh, Wkl = W0h, W0l
        Wrh, Wrl = gate_weights("Wr")
        E1h, E1l = sb("E1h", [P, E + 1, K * HID], F16), sb("E1l", [P, E + 1, K * HID], F16)
        E2h, E2l = sb("E2h", [P, E + 1, FC * D], F16), sb("E2l", [P, E + 1, FC * D], F16)
        I64 = sb("I64", [P, P], F16)
        cond = sb("cond", [P, K, B])
        v0 = temp(3 * K * B).rearrange("p (g b) -> p g b", b=B)
        v0_parts = temp(3 * K * B).bitcast(F16).rearrange("p (h n) -> p h n", h=2)
        b0s = sb("b0s", [P, 3 * K])
        b1s = sb("b1s", [P, 3 * K])
        eb1s = sb("eb1s", [P, (E + 1) * FC])
        h_parts = sb("h_parts", [P, 2, K * B], F16)
        hh_, hl_ = h_parts[:, 0, :], h_parts[:, 1, :]
        rhh, rhl, rh32 = sb("rh_hi", [P, K * B], F16), sb("rh_lo", [P, K * B], F16), temp(K * B)
        gr, gz = sb("gr", [P, K * B]), sb("gz", [P, K * B])
        fma_m, fma_ab = (temp(2 * K * B).rearrange("p (j s) -> p j s", s=2) for _ in range(2))
        cell_buf = sb("cell_buf", [P, 2 * (5 * K * B + 2)])
        cell_add, cell_mul = (cell_buf[:, n * 5 * K * B:(n + 1) * 5 * K * B].rearrange("p (j s) -> p j s", s=5) for n in range(2))
        cell_gates = cell_buf[:, :].rearrange("p (g n) -> p g n", g=2)[:, :, 0:5 * K * B]\
            .rearrange("p g (j s) -> p g j s", s=5)[:, :, :, 0]
        cells = sb("cells", [P, K * B, 5])
        gf_sum, o_sum = sb("gf_sum", [P, 2 * K, B]), sb("o_sum", [P, K, B])
        hs32, hs16 = temp(4 * K * B).rearrange("p (i j s) -> p i j s", i=2, s=2), sb("hs16", [P, K * B, 2], F16)
        h32 = sb("h32", [P, 2, K * B])
        zeros, eps, mark = sb("zeros", [P, T]), sb("eps", [P, 1]), sb("mark", [P, 8])
        tcell = sb("tcell", [P, K * B])
        sgc, silu = sb("sgc", [P, K, B]), sb("silu", [P, K, B])
        gws = sb("gws", [P, 3 * K, E])
        tws = sb("tws", [P, K, 2 * E])
        sbb = sb("sbb", [B, 3 * E])
        part = sb("part", [P, T, 3])
        part9 = sb("part9", [P, 3, 3, K * B])
        seg = sb("seg", [P, 3, K * B])
        agg = sb("agg", [P, 3, K * B])
        lg, mod, ex, sc = sb("lg", [B, E]), sb("mod", [B, 2 * E]), sb("ex", [B, E]), sb("sc", [B, E])
        mx, sm, rs = sb("mx", [B, 1]), sb("sm", [B, 1]), sb("rs", [B, 1])
        g3, q3, low = sb("g3", [B, E, E]), sb("q3", [B, E, E]), sb("low", [B, E * E])
        rank, sel5 = sb("rank", [B, E]), sb("sel5", [B, E + 1])
        bs = sb("bs", [B, P])
        mtok, wtok = sb("mtok", [P, N_TILES, E]), sb("wtok", [P, N_TILES, E])
        eb2b = sb("eb2b", [P, E + 1, D])
        bank = [ctx.enter_context(nc.psum_tensor(f"bank{i}", [P, 512], F32)) for i in range(8)]

        in_w0, in_u0, in_small, in_late = sem("in_w0"), sem("in_u0"), sem("in_small"), sem("in_late")
        in_x = [sem(f"in_x{i}") for i in range(N_LOADS)]
        staged = [sem(f"staged{i}") for i in range(N_STAGE)]
        stage_free = sem("stage_free")
        out_done = sem("out_done")
        dve_step, pool_step = sem("dve_step"), sem("pool_step")
        wtok_ready, pool_row, pool_out_ready = sem("wtok_ready"), sem("pool_row"), sem("pool_out_ready")
        w0_hi, u0_hi, w0_ready, u0_ready, x0_ready = (sem(n) for n in ("w0_hi", "u0_hi", "w0_ready", "u0_ready", "x0_ready"))
        v_psum, v_ready = sem("v_psum"), sem("v_ready")
        r_psum, z_psum, hh_psum = sem("r_psum"), sem("z_psum"), sem("hh_psum")
        r_sig, z_sig, hh_tanh = sem("r_sig"), sem("z_sig"), sem("hh_tanh")
        rh_hi_ready, rh_32_ready, rh_lo_ready = sem("rh_hi_ready"), sem("rh_32_ready"), sem("rh_lo_ready")
        h_hi_ready, h_32_ready, h_lo_ready = sem("h_hi_ready"), sem("h_32_ready"), sem("h_lo_ready")
        zh_ready, x1_added = sem("zh_ready"), sem("x1_added")
        last_info, suffix_ready, weighted_ready = sem("last_info"), sem("suffix_ready"), sem("weighted_ready")
        x1_ready, last_psum, last_gates, last_norm, last_decay, sgc_ready, hidden_ready = (sem(n) for n in (
            "x1_ready", "last_psum", "last_gates", "last_norm", "last_decay", "sgc_ready", "hidden_ready"))
        x2_double, x2_hi, x2_parts, x3_hi = sem("x2_double"), sem("x2_hi"), sem("x2_parts"), sem("x3_hi")
        gf_psum, o_psum, gf_tanh, o_tanh, c_tanh = (sem(n) for n in ("gf_psum", "o_psum", "gf_tanh", "o_tanh", "c_tanh"))
        gf_ready, o_ready = sem("gf_ready"), sem("o_ready")
        c_ready = sem("c_ready")
        s_hi_ready, s_32_ready, s_lo_ready = sem("s_hi_ready"), sem("s_32_ready"), sem("s_lo_ready")
        x3_added, x3_split = sem("x3_added"), sem("x3_split")
        up_psum, gelu_ready, gh_ready, gl_ready, down_done = (sem(n) for n in (
            "up_psum", "gelu_ready", "gh_ready", "gl_ready", "down_done"))
        part_ready, silu_ready, agg_ready, gate_psum = (sem(n) for n in (
            "part_ready", "silu_ready", "agg_ready", "gate_psum"))
        mx_ready, ex_ready, sel_ready, wsel_psum, y_ready, out_ready = (sem(n) for n in (
            "mx_ready", "ex_ready", "sel_ready", "wsel_psum", "y_ready", "out_ready"))

        block = ctx.enter_context(nc.Block())

        flat = lambda t: t.rearrange("p a n -> p (a n)")
        flat4 = lambda t: t[:, :, :, :].rearrange("p g k n -> p (g k n)")
        pieces = []
        for src, hi, lo, n, doubled in ((w1, flat4(W1h), flat4(W1l), 3 * K * D, 0),
                                        (wr, flat4(Wrh), flat4(Wrl), 3 * K * D, DOUBLED),
                                        (ew1, flat(E1h[:, :, :]), flat(E1l[:, :, :]), (E + 1) * K * HID, 0),
                                        (ew2, flat(E2h[:, :, :]), flat(E2l[:, :, :]), (E + 1) * FC * D, 0),
                                        (wk, flat4(Wkh), flat4(Wkl), 3 * K * D, DOUBLED)):
            ends = [0, doubled] if doubled else [0]
            while ends[-1] < n:
                ends.append(min(n, ends[-1] + STAGE))
            for a, z in zip(ends, ends[1:]):
                pieces.append((src[:, a:z], hi[:, a:z], lo[:, a:z], z - a, SPLIT_SCALE * (2 if z <= doubled else 1)))
        first_wk = len(pieces) - 2
        stage_u0 = pre[:, 0:3 * K * D]
        stage_w0 = pre[:, 3 * K * D:2 * 3 * K * D]
        stage_c0 = flat_stage[:, 0:3 * K * D].rearrange("p (g k n) -> p g k n", g=3, k=K)

        @block.sync
        def _(sp):
            sp.dma_start(stage_w0, w0).then_inc(in_w0, 16)
            for i in range(N_LOADS):
                cols = slice(i * NT, (i + 1) * NT)
                sp.dma_start(X[:, :, cols], xT[:, :, cols]).then_inc(in_x[i], 16)
                if i == 0:
                    sp.dma_start(stage_c0, c0).then_inc(in_small, 16)
                    for dst, src in ((cond[:, :, :], condT), (b0s[:, :], b0), (I[:, :], ident)):
                        sp.dma_start(dst, src).then_inc(in_small, 16)
                    sp.dma_start(stage_u0, u0).then_inc(in_u0, 16)
            for dst, src in ((b1s[:, :], b1), (eb1s[:, :], eb1), (eb2b[:, :, :], eb2), (gws[:, :, :], gate_w),
                             (tws[:, :, :], time_w), (sbb[:, :], small_b), (low[:, :], lower), (bs[:, :], bsel),
                             (mtok[:, :, :], mask_tok)):
                sp.dma_start(dst, src).then_inc(in_late, 16)
            sp.wait_ge(v_psum, 1)
            for n, (src, _, _, m, _) in enumerate(pieces):
                if n >= N_STAGE:
                    sp.wait_ge(stage_free, n - N_STAGE + 1)
                sp.dma_start(stage[:, n % N_STAGE, 0:m], src).then_inc(staged[n % N_STAGE], 16)
            for r in range(N_TILES):
                if r in BY_POOL:
                    sp.wait_ge(pool_out_ready, BY_POOL.index(r) + 1)
                else:
                    sp.wait_ge(out_ready, r + 1 - sum(i < r for i in BY_POOL))
                sp.dma_start(out[:, r * TS:(r + 1) * TS, :].rearrange("b t d -> t b d"),
                             rows_last[:, r * TS:(r + 1) * TS, :].rearrange("p t c -> p (t c)")).then_inc(out_done, 16)
            sp.wait_ge(out_done, 16 * N_TILES)

        flat3 = lambda t: t.rearrange("p a c -> p (a c)")

        def halves(t):
            return t.rearrange("p (k b) -> p k b", k=K)

        def routed_rows(t0, m):
            if m < E:
                return flat3(rows_y[:, bass.ds(t0, TS), :])[:, (m - 1) * D:m * D]
            return flat3(rows_last[:, bass.ds(t0, TS), :])

        @block.gpsimd
        def _(pool):
            for n, (_, hi, lo, m, scale) in enumerate(pieces):
                src = stage[:, n % N_STAGE, 0:m]
                pool.wait_ge(staged[n % N_STAGE], 16 * (n // N_STAGE + 1))
                nc.gpsimd.tensor_scalar(src, src, scale, 1.0, ALU.mult, ALU.mult).then_inc(pool_step, 1)
                pool.wait_ge(pool_step, 2 * n + 1)
                if n == first_wk:
                    pool.wait_ge(hh_psum, T)
                nc.gpsimd.tensor_copy(hi, src).then_inc(pool_step, 1)
                pool.wait_ge(pool_step, 2 * n + 2)
                nc.gpsimd.tensor_tensor(lo, src, hi, ALU.subtract).then_inc(stage_free, 1)

            def double_parts(t, c):
                hi, lo = x_parts[:, c % 2, 0], x_parts[:, c % 2, 1]
                x = X[:, :, bass.ds(t * B, CC)]
                nc.gpsimd.tensor_tensor(x_double[:, :, :], x, x, ALU.add)\
                    .then_inc(x2_double, CH)
                pool.wait_ge(x2_double, t)
                nc.gpsimd.tensor_copy(hi, x_double[:, :, :]).then_inc(x2_hi, CH)
                pool.wait_ge(x2_hi, t + CH)
                nc.gpsimd.tensor_tensor(lo, x_double[:, :, :], hi, ALU.subtract).then_inc(x2_parts, CH)
                pool.wait_ge(x2_parts, t + CH)

            pool.wait_ge(hidden_ready, 2 * CH)
            double_parts(CH, 1)
            pool.wait_ge(hidden_ready, 3 * CH)
            pool.wait_ge(o_psum, 1)
            double_parts(2 * CH, 2)
            pool.wait_ge(o_psum, CH)
            double_parts(3 * CH, 3)
            pool.wait_ge(hidden_ready, T)
            with pool.Fori(4 * CH, T - PAIR + 1, PAIR) as t0:
                for c in range(2):
                    pool.wait_ge(o_psum, t0 + (c - 2) * CH)
                    double_parts(t0 + c * CH, c)
            nc.gpsimd.memset(mark[:, 7:8], 0.0).then_inc(x2_parts, CH)
            pool.wait_ge(wtok_ready, 1)
            count = 0
            for i in BY_POOL:
                row = X[:, :, i * TC:(i + 1) * TC]
                ys = [halves(routed_rows(i * TS, m)) for m in networks(i)[1:]]
                for n, y in enumerate(ys):
                    m = networks(i)[1:][n]
                    nc.gpsimd.tensor_scalar(y, y, wtok[:, i, m - 1:m], 1.0, ALU.mult, ALU.mult).then_inc(pool_row, 1)
                count += len(ys)
                for y in ys:
                    pool.wait_ge(pool_row, count)
                    ins = nc.gpsimd.tensor_tensor(y if y is ys[-1] else row, y, row, ALU.add)
                    if y is not ys[-1]:
                        count += 1
                        ins.then_inc(pool_row, 1)
                ins.then_inc(pool_out_ready, 1)

        def project(out_, wh, wl, gate, m, parts, start):
            cols = slice(m * P, (m + 1) * P)
            for k in range(K):
                for n, (w, h) in enumerate(((wh, 0), (wl, 0), (wh, 1))):
                    last = nc.tensor.matmul(out_, w[:, gate, k, cols], parts[:, h, k, :].rearrange("p (t b) -> p t b", b=B),
                                            start=start and k == 0 and n == 0, stop=False, skip_group_check=True)
            return last

        chunk_bank = lambda n: bank[n][:, 0:CC * K].rearrange("p (t m b) -> p t m b", t=CH, m=K)
        RZH = [[chunk_bank(2 * g + c) for g in range(3)] for c in range(2)]
        GF, O = ([bank[n][:, 0:CH * gates * K * 2 * B].rearrange("p (t g h b) -> p t g h b", t=CH, h=2, b=B) for n in banks]
                 for gates, banks in ((2, (2, 3)), (1, (4, 7))))
        P1 = [bank[6 + n][:, 0:CC].rearrange("p (t b) -> p t b", b=B) for n in range(2)]
        L1_ORDER = ((0, 0), (1, 0), (0, 1), (1, 1), (2, 0), (2, 1))

        def gate_products(psum, wh, wl, a, gate, part, blocks=range(K)):
            for m in blocks:
                for k in range(K):
                    for w in ((wh, wl) if part == "hi" else (wh,)):
                        last = nc.tensor.matmul(psum[:, m, :], w[:, gate, k, m * P:(m + 1) * P], a[:, k * B:(k + 1) * B],
                                                start=False, stop=False, skip_group_check=True)
            return last

        def blocks_of(s, nets):
            blocks = [(p, m, f) for p, m in enumerate(nets) for f in range(FC)]
            n = LAST_UP + 1
            return blocks[s * len(blocks) // n:(s + 1) * len(blocks) // n] if 0 <= s < n else []

        segments = []
        for i in range(N_TILES - 1):
            if segments and segments[-1][2] == networks(i):
                segments[-1][1] += TS
            else:
                segments.append([(i + 1) * TS, (i + 2) * TS, networks(i)])

        def over_tiles(engine, tile):
            for a, z, nets in segments:
                if (z - a) // TS % 2:
                    tile(a, nets, a // TS % 2)
                    a += TS
                if z > a:
                    with engine.Fori(a, z - 2 * TS + 1, 2 * TS) as t0:
                        for i in range(2):
                            tile(t0 + i * TS, nets, (a // TS + i) % 2)

        @block.tensor
        def _(pe):
            pe.wait_ge(in_small, 64)
            for g in range(3 * K):
                for k in range(K):
                    last = nc.tensor.matmul(bank[7][:, g * B:(g + 1) * B],
                                            stage_c0[:, g // K, k, g % K * P:(g % K + 1) * P], cond[:, k, :],
                                            start=k == 0, stop=k == K - 1)
            last.then_inc(v_psum, 1)

            def condition0(c, g):
                for h in range(2):
                    v = v0_parts[:, h:h + 1, g * K * B:(g + 1) * K * B]
                    nc.tensor.matmul(bank[2 * g + c % 2][:, 0:CC * K].rearrange("p (t n) -> p t n", t=CH), I64[:, :],
                                     v.broadcast_to([P, CH, K * B]), start=h == 0, stop=False, skip_group_check=True)

            def project0(c, g, m):
                project(RZH[c % 2][g][:, :, m, :], W0h, W0l, g, m, x_parts[:, c % 2], start=False)

            def project1(n):
                g, m = L1_ORDER[n]
                return project(P1[n % 2], W1h, W1l, g, m, x1_parts, start=True)

            def chunk0(t0, c):
                for u in range(CH):
                    t = t0 + u
                    R, Z, H = (RZH[c % 2][g][:, u] for g in range(3))
                    h16 = hs16[:, :, 1]
                    pe.wait_ge(h_hi_ready, t + 1)
                    gate_products(R, U0h, U0l, h16, 0, "hi")
                    pe.wait_ge(h_lo_ready, t + 1)
                    gate_products(R, U0h, U0l, hl_, 0, "lo").then_inc(r_psum, 1)
                    gate_products(Z, U0h, U0l, h16, 1, "hi")
                    gate_products(Z, U0h, U0l, hl_, 1, "lo").then_inc(z_psum, 1)
                    ahead = c < T // CH - 1
                    if ahead and 1 <= u <= 3 * K:
                        project0(c + 1, (u - 1) // K, (u - 1) % K)
                    pe.wait_ge(rh_hi_ready, t + 1)
                    gate_products(H, U0h, U0l, rhh, 2, "hi")
                    pe.wait_ge(rh_lo_ready, t + 1)
                    gate_products(H, U0h, U0l, rhl, 2, "lo").then_inc(hh_psum, 1)
                    if ahead and u < 2:
                        for g in ((0, 1), (2,))[u]:
                            condition0(c + 1, g)
                    if c >= 1 and 1 <= u <= 3 * K:
                        if c == 1 and u == 1:
                            pe.wait_ge(stage_free, 2)
                        project1(u - 1)

            pe.wait_ge(w0_ready, 1)
            pe.wait_ge(x0_ready, 1)
            pe.wait_ge(v_ready, 1)
            for g in range(3):
                condition0(0, g)
                for m in range(K):
                    project0(0, g, m)
            pe.wait_ge(u0_ready, 1)
            for c in range(2):
                chunk0(c * CH, c)
            with pe.Fori(PAIR, T - 2 * PAIR + 1, PAIR) as t0:
                for c in range(2):
                    chunk0(t0 + c * CH, 2 + c)
            for c in range(T // CH - 2, T // CH):
                chunk0(c * CH, c)
            pe.wait_ge(x1_ready, 1)
            for n in range(3 * K):
                if n >= 1:
                    pe.wait_ge(last_gates, n)
                project1(n).then_inc(last_psum, 1)

            def project2(c, n):
                g, m = divmod(n, K)
                banks, at = (GF, n) if g < 2 else (O, m)
                project(banks[c % 2][:, :, at, 0, :], Wkh, Wkl, g, m, x_parts[:, c % 2], start=at == 0)

            def step2(t, s):
                c, u = divmod(s, CH)
                step_gf, step_o = GF[c % 2][:, u], O[c % 2][:, u]

                def low_weights(psum, gate, blocks):
                    for m in blocks:
                        for k in range(K):
                            nc.tensor.matmul(psum[:, (gate % 2) * K + m, 0, :], Wrl[:, gate, k, m * P:(m + 1) * P],
                                             hh_[:, k * B:(k + 1) * B], start=False, stop=False, skip_group_check=True)

                def high_weights(psum, gate):
                    for m in range(K):
                        for k in range(K):
                            last = nc.tensor.matmul(psum[:, (gate % 2) * K + m], Wrh[:, gate, k, m * P:(m + 1) * P],
                                                    h_parts[:, :, k * B:(k + 1) * B], start=False, stop=False,
                                                    skip_group_check=True)
                    return last

                pe.wait_ge(s_hi_ready, t + 1)
                low_weights(step_gf, 0, range(K))
                low_weights(step_gf, 1, range(K))
                low_weights(step_o, 2, range(1))
                pe.wait_ge(s_lo_ready, t + 1)
                high_weights(step_gf, 0)
                high_weights(step_gf, 1).then_inc(gf_psum, 1)
                low_weights(step_o, 2, range(1, K))
                high_weights(step_o, 2).then_inc(o_psum, 1)
                if 1 <= u <= 3 * K:
                    if u == 1:
                        pe.wait_ge(x2_parts, t + (2 * CH - u))
                    project2(c + 1, u - 1)

            pe.wait_ge(stage_free, len(pieces))
            pe.wait_ge(x2_parts, CH)
            for n in range(3 * K):
                project2(0, n)

            def up(s, j, m, f, x):
                out_ = bank[s % 2][:, j * TC:(j + 1) * TC]
                for k in range(K):
                    cols = slice(k * HID + f * P, k * HID + (f + 1) * P)
                    for n, (w, h) in enumerate(((E1h, 0), (E1l, 0), (E1h, 1))):
                        last = nc.tensor.matmul(out_, w[:, m, cols], x[:, h, k, :],
                                                start=k == 0 and n == 0, stop=k == K - 1 and n == 2)
                return last

            def down(s, j, p, m, f, x):
                acc = bank[5 + p % 2][:, 0:D]
                for n, (part, w) in enumerate(((Gh, E2h), (Gh, E2l), (Gl, E2h))):
                    last = nc.tensor.matmul(acc, part[:, s % 2, j, :], w[:, m, f * D:(f + 1) * D],
                                            start=f == 0 and n == 0, stop=False, skip_group_check=True)
                if m == 0 and f == 0:
                    for k in range(K):
                        for h in range(2):
                            last = nc.tensor.matmul(acc[:, k * P:(k + 1) * P], x[:, h, k, :], I64[:, :],
                                                    start=False, stop=False, skip_group_check=True)
                return last

            def step3(t, s, nets, x):
                if s == 0:
                    pe.wait_ge(x3_split, t)
                blocks = blocks_of(s, nets)
                if blocks:
                    pe.wait_ge(gelu_ready, t - 1)
                    for j, (_, m, f) in enumerate(blocks):
                        last = up(s, j, m, f, x)
                    last.then_inc(up_psum, 2 if s == LAST_UP else 1)
                blocks = blocks_of(s - 1, nets)
                if blocks:
                    pe.wait_ge(gl_ready, t)
                    for j, (p, m, f) in enumerate(blocks):
                        last = down(s - 1, j, p, m, f, x)
                    last.then_inc(down_done, 2 if s == 1 else 1)

            def routing_products():
                pe.wait_ge(in_late, IN_LATE)
                pe.wait_ge(silu_ready, 1)
                for k in range(K):
                    nc.tensor.matmul(bank[2][0:B, 0:2 * E], silu[:, k, :], tws[:, k, :], start=k == 0, stop=k == K - 1)
                pe.wait_ge(agg_ready, 1)
                for a in range(3):
                    for k in range(K):
                        last = nc.tensor.matmul(bank[3][0:B, 0:E], agg[:, a, k * B:(k + 1) * B], gws[:, a * K + k, :],
                                                start=a == 0 and k == 0, stop=a == 2 and k == K - 1)
                last.then_inc(gate_psum, 1)

            for s in range(TS):
                step2(s, s)

            def tile(t0, nets, parity):
                for s in range(TS):
                    step2(t0 + s, s)
                    step3(t0 + s, s, nets, x3_parts[:, 1 - parity])

            over_tiles(pe, tile)
            for s in range(TS):
                step3(T + s, s, networks(N_TILES - 1), x3_parts[:, (N_TILES - 1) % 2])
                if s == 0:
                    routing_products()
                if s == ROUTED:
                    pe.wait_ge(sel_ready, 1)
                    nc.tensor.matmul(bank[4][:, 0:E], bs[:, :], sel5[:, 0:E], start=True, stop=True).then_inc(wsel_psum, 1)

        @block.scalar
        def _(act):
            nc.scalar.preload_act_table(ACT.Sigmoid)
            act.wait_ge(in_w0, 16)
            nc.scalar.activation(flat4(W0h), stage_w0, ACT.Identity, scale=SPLIT_SCALE).then_inc(w0_hi, 1)
            act.wait_ge(in_small, 64)
            nc.scalar.activation(sgc[:, :, :], cond[:, :, :], ACT.Sigmoid).then_inc(sgc_ready, 1)
            act.wait_ge(in_u0, 16)
            nc.scalar.activation(flat4(U0h), stage_u0, ACT.Identity, scale=SPLIT_SCALE).then_inc(u0_hi, 1)

            def gate1(n):
                g, m = L1_ORDER[n]
                dst = (f_c, i_c, c_c)[g][:, m, :].rearrange("p (t b) -> p t b", b=B)
                return nc.scalar.activation(dst, P1[n % 2], ACT.Sigmoid if g < 2 else ACT.Identity,
                                            bias=b1s[:, g * K + m:g * K + m + 1], scale=UNSCALE)

            def guarded(dst):
                src = norm_f[:, :, :].rearrange("p k (t b) -> p k b t", b=B)
                return nc.scalar.activation(dst.rearrange("p (k b) t -> p k b t", k=K), src, ACT.Identity, bias=eps[:, 0:1])

            def chunk0(t0, c):
                for u in range(CH):
                    t = t0 + u
                    R, Z, H = (RZH[c % 2][g][:, u].rearrange("p m b -> p (m b)") for g in range(3))
                    act.wait_ge(r_psum, t + 1)
                    nc.scalar.activation(gr[:, :], R, ACT.Sigmoid, scale=UNSCALE).then_inc(r_sig, 1)
                    act.wait_ge(z_psum, t + 1)
                    nc.scalar.activation(fma_m[:, :, 1], Z, ACT.Sigmoid, scale=UNSCALE).then_inc(z_sig, 1)
                    act.wait_ge(hh_psum, t + 1)
                    nc.scalar.activation(fma_ab[:, :, 0], H, ACT.Tanh, scale=UNSCALE).then_inc(hh_tanh, 1)
                    if c >= 1 and u >= 2:
                        if c == 1 and u == 2:
                            act.wait_ge(in_late, IN_LATE)
                        ins = gate1(u - 2)
                        if c == T // CH - 1 and u == CH - 1:
                            ins.then_inc(last_gates, 1)
                    if c >= 2 and u == 2:
                        guarded(decay_m[:, :, 1:])
                    if c >= 2 and u == 3:
                        guarded(bufG[:, :, bass.ds(t0 - 2 * CH, CH)])

            for c in range(2):
                chunk0(c * CH, c)
            with act.Fori(PAIR, T - 2 * PAIR + 1, PAIR) as t0:
                for c in range(2):
                    chunk0(t0 + c * CH, 2 + c)
            for c in range(T // CH - 2, T // CH):
                chunk0(c * CH, c)
            act.wait_ge(last_norm, 1)
            guarded(decay_m[:, :, 1:])
            guarded(bufG[:, :, T - 2 * CH:T - CH]).then_inc(last_decay, 1)
            act.wait_ge(last_info, 1)
            for n in range(3 * K):
                act.wait_ge(last_psum, n + 1)
                gate1(n).then_inc(last_gates, 1)
            nc.scalar.preload_act_table(ACT.Gelu_apprx_tanh)
            act.wait_ge(last_norm, 2)
            guarded(decay_m[:, :, 1:])
            guarded(bufG[:, :, T - CH:T]).then_inc(last_decay, 1)

            def step2(t):
                act.wait_ge(gf_ready, t + 1)
                gates = gf_sum[:, :, :].rearrange("p (g m) b -> p g (m b)", g=2)
                nc.scalar.activation(cell_gates, gates, ACT.Tanh, scale=UNSCALE / 4)
                nc.scalar.activation(cell_add[:, :, 3], gates[:, 0], ACT.Tanh, scale=UNSCALE / 4).then_inc(gf_tanh, 1)
                act.wait_ge(o_ready, t + 1)
                nc.scalar.activation(gz[:, :], flat(o_sum[:, :, :]), ACT.Tanh, scale=UNSCALE / 4).then_inc(o_tanh, 1)
                act.wait_ge(c_ready, t + 1)
                nc.scalar.activation(tcell[:, :], cells[:, :, 4], ACT.Tanh).then_inc(c_tanh, 1)

            def step3(t, s, nets):
                blocks = blocks_of(s, nets)
                if blocks:
                    act.wait_ge(up_psum, t + 1)
                    act.wait_ge(gl_ready, t - 1)
                    for j, (_, m, f) in enumerate(blocks):
                        last = nc.scalar.activation(G[:, s % 2, j, :], bank[s % 2][:, j * TC:(j + 1) * TC],
                                                    ACT.Gelu_apprx_tanh, bias=eb1s[:, m * FC + f:m * FC + f + 1],
                                                    scale=UNSCALE)
                    last.then_inc(gelu_ready, 2 if s == LAST_UP else 1)

            for s in range(TS):
                step2(s)

            def tile(t0, nets, _):
                for s in range(TS):
                    step2(t0 + s)
                    step3(t0 + s, s, nets)

            over_tiles(act, tile)
            for s in range(TS):
                if s == 1:
                    act.wait_ge(mx_ready, 1)
                    nc.scalar.activation(ex[:, :], lg[:, :], ACT.Exp, bias=mx[:, 0:1]).then_inc(ex_ready, 1)
                    nc.scalar.preload_act_table(ACT.Gelu_apprx_tanh)
                step3(T + s, s, networks(N_TILES - 1))

        @block.vector
        def _(dve):
            steps = [0]

            def then_wait(ins):
                steps[0] += 1
                ins.then_inc(dve_step, 1)
                dve.wait_ge(dve_step, steps[0])

            nc.vector.memset(zeros[:, :], 0.0)
            nc.vector.memset(eps[:, :], EPS)
            for n, begun in enumerate((up_psum, gelu_ready, gh_ready, gl_ready, down_done)):
                nc.vector.memset(mark[:, n:n + 1], 0.0).then_inc(begun, TS)
            nc.vector.memset(fma_m, 0.0)
            then_wait(nc.vector.memset(cell_buf[:, :], 0.0))
            for slot, factor in ((1, -1.0), (3, 1.0), (4, 0.5)):
                nc.vector.memset(cell_mul[:, :, slot], factor)
            nc.vector.memset(decay_m[:, :, :], 0.0)
            then_wait(nc.vector.memset(decay_a[:, :, :], 0.0))
            nc.vector.memset(hs32, 0.0).then_inc(h_32_ready, 1)
            nc.vector.memset(hs16[:, :, :], 0.0).then_inc(h_hi_ready, 1)
            nc.vector.memset(hl_, 0.0).then_inc(h_lo_ready, 1)
            dve.wait_ge(in_w0, 16)
            dve.wait_ge(w0_hi, 1)
            nc.vector.scalar_tensor_tensor(flat4(W0l), stage_w0, SPLIT_SCALE, flat4(W0h), ALU.mult, ALU.subtract)\
                .then_inc(w0_ready, 1)

            def x0_hi(t, c):
                return nc.vector.tensor_copy(x_parts[:, c % 2, 0], X[:, :, bass.ds(t * B, CC)])

            def x0_lo(t, c):
                return nc.vector.tensor_tensor(x_parts[:, c % 2, 1], X[:, :, bass.ds(t * B, CC)], x_parts[:, c % 2, 0],
                                               ALU.subtract)

            dve.wait_ge(in_x[0], 16)
            then_wait(x0_hi(0, 0))
            x0_lo(0, 0).then_inc(x0_ready, 1)
            then_wait(x0_hi(CH, 1))
            x0_lo(CH, 1)
            dve.wait_ge(in_small, 64)
            nc.vector.tensor_scalar(I64[:, :], I[:, :], SPLIT_SCALE, None, ALU.mult)
            nc.vector.tensor_copy(decay_a[:, :, 0], flat(cond[:, :, :]))
            dve.wait_ge(v_psum, 1)
            then_wait(nc.vector.tensor_tensor(v0, bank[7][:, 0:3 * K * B].rearrange("p (g b) -> p g b", b=B),
                                              b0s[:, :, None].broadcast_to([P, 3 * K, B]), ALU.add))
            then_wait(nc.vector.tensor_copy(v0_parts[:, 0, :], flat(v0)))
            nc.vector.tensor_tensor(v0_parts[:, 1, :], flat(v0), v0_parts[:, 0, :], ALU.subtract)\
                .then_inc(v_ready, 1)
            dve.wait_ge(in_u0, 16)
            dve.wait_ge(u0_hi, 1)
            nc.vector.scalar_tensor_tensor(flat4(U0l), stage_u0, SPLIT_SCALE, flat4(U0h), ALU.mult, ALU.subtract)\
                .then_inc(u0_ready, 1)

            def fma(out_):
                return nc.vector.tensor_tensor_scan(out_, flat3(fma_m), flat3(fma_ab), 0.0,
                                                    ALU.mult, ALU.add)

            def x1_hi(t):
                return nc.vector.tensor_tensor(x1_parts[:, 0], X[:, :, bass.ds(t * B, CC)], halves(zeros[:, 0:K * CC]), ALU.add)

            def x1_lo(t):
                return nc.vector.tensor_tensor(x1_parts[:, 1], X[:, :, bass.ds(t * B, CC)], x1_parts[:, 0], ALU.subtract)

            def gate_sum(k):
                return nc.vector.scalar_tensor_tensor(sum_c[:, k, :], f_c[:, k, :], EPS, i_c[:, k, :], ALU.add, ALU.add)

            def gate_inverse(k):
                return nc.vector.reciprocal(sum_c[:, k, :], sum_c[:, k, :])

            def normal_f():
                return nc.vector.tensor_tensor(norm_f, f_c, sum_c, ALU.mult)

            def normal_i():
                return nc.vector.tensor_tensor(norm_i, i_c, sum_c, ALU.mult)

            by_b = lambda ap: ap.rearrange("p k (t b) -> p k b t", b=B)

            def new_info(t):
                return nc.vector.tensor_tensor(bufI[:, :, bass.ds(t, CH)].rearrange("p (k b) t -> p k b t", k=K),
                                               by_b(norm_i), by_b(c_c), ALU.mult)

            def decay_scan():
                return nc.vector.tensor_tensor_scan(flat3(decay), flat3(decay_m), flat3(decay_a), 0.0, ALU.mult, ALU.add)

            def decay_carry():
                return nc.vector.tensor_copy(decay_a[:, :, 0], decay[:, :, CH])

            def add_decay(t):
                x = by_b(X[:, :, bass.ds(t * B, CC)])
                return nc.vector.tensor_tensor(x, x, decay[:, :, 1:].rearrange("p (k b) t -> p k b t", k=K), ALU.add)

            def between(u, place, t0, c):
                x1, gates, tail, ahead = c >= 1, c >= 1, c >= 2, c < T // CH - 2
                if place == 0:
                    if u == 0 and x1:
                        x1_lo(t0 - CH)
                    if u == 1 and tail:
                        normal_f()
                    if u == 2 and tail:
                        new_info(t0 - 2 * CH)
                    if u == 3 and tail:
                        decay_scan()
                    if u == 4 and gates:
                        gate_sum(0)
                    if u == 5 and tail:
                        decay_carry()
                    if u == 6 and gates:
                        gate_sum(1)
                else:
                    if u == 1 and tail:
                        normal_i()
                    if u == 2 and ahead:
                        x0_hi(t0 + 2 * CH, c)
                    if u == 3 and tail:
                        add_decay(t0 - 2 * CH)
                    if u == 5 and ahead:
                        x0_lo(t0 + 2 * CH, c)
                    if u == 4 and gates:
                        gate_inverse(0)
                    if u == 6 and gates:
                        gate_inverse(1)
                    if u == 7:
                        x1_hi(t0)

            def chunk0(t0, c):
                for u in range(CH):
                    t = t0 + u
                    h, new = hs32[:, u % 2, :, 1], hs32[:, (u + 1) % 2]
                    dve.wait_ge(r_sig, t + 1)
                    nc.vector.tensor_tensor(rhh[:, :], gr[:, :], h, ALU.mult).then_inc(rh_hi_ready, 1)
                    nc.vector.tensor_tensor(rh32, gr[:, :], h, ALU.mult).then_inc(rh_32_ready, 1)
                    dve.wait_ge(rh_32_ready, t + 1)
                    nc.vector.tensor_tensor(rhl[:, :], rh32, rhh[:, :], ALU.subtract).then_inc(rh_lo_ready, 1)
                    dve.wait_ge(z_sig, t + 1)
                    nc.vector.scalar_tensor_tensor(fma_ab[:, :, 1], fma_m[:, :, 1], 1.0, h, ALU.subtract, ALU.mult,
                                                   reverse0=True).then_inc(zh_ready, 1)
                    between(u, 0, t0, c)
                    dve.wait_ge(hh_tanh, t + 1)
                    dve.wait_ge(zh_ready, t + 1)
                    fma(flat3(hs16[:, :, :])).then_inc(h_hi_ready, 1)
                    fma(flat3(new)).then_inc(h_32_ready, 1)
                    dve.wait_ge(h_32_ready, t + 2)
                    nc.vector.tensor_tensor(hl_, new[:, :, 1], hs16[:, :, 1], ALU.subtract).then_inc(h_lo_ready, 1)
                    xs = X[:, :, bass.ds(t * B, B)]
                    nc.vector.tensor_tensor(xs, xs, halves(new[:, :, 1]), ALU.add).then_inc(x1_added, 1)
                    if u == CH - 1:
                        dve.wait_ge(x1_added, t + 1)
                    between(u, 1, t0, c)

            for c in range(2):
                chunk0(c * CH, c)
            for i in range(1, N_LOADS):
                dve.wait_ge(in_x[i], 16)
            with dve.Fori(PAIR, T - 2 * PAIR + 1, PAIR) as t0:
                for c in range(2):
                    chunk0(t0 + c * CH, 2 + c)
            for c in range(T // CH - 2, T // CH):
                chunk0(c * CH, c)

            def last_tail(n, t):
                then_wait(normal_i())
                if n == 1:
                    dve.wait_ge(last_gates, 1)
                new_info(t).then_inc(last_info, 1)
                dve.wait_ge(last_decay, n)
                then_wait(decay_scan())
                add_decay(t)
                then_wait(decay_carry())

            normal_f().then_inc(last_norm, 1)
            dve.wait_ge(last_norm, 1)
            x1_lo(T - CH).then_inc(x1_ready, 1)
            last_tail(1, T - 2 * CH)
            dve.wait_ge(last_gates, 1 + 4)
            for k in range(K):
                then_wait(gate_sum(k))
            for k in range(K):
                then_wait(gate_inverse(k))
            normal_f().then_inc(last_norm, 1)
            dve.wait_ge(last_gates, 1 + 3 * K)
            last_tail(2, T - CH)

            rows = lambda k: range(k * B, (k + 1) * B)
            for k in range(K):
                for j in rows(k):
                    ins = nc.vector.tensor_tensor_scan(bufG[:, j, ::-1], bufG[:, j, ::-1], zeros[:, :], 1.0,
                                                       ALU.mult, ALU.add)
                if k == 0:
                    ins.then_inc(suffix_ready, 1)
            ins.then_inc(suffix_ready, 1)
            for k in range(K):
                dve.wait_ge(suffix_ready, k + 1)
                half = slice(k * B, (k + 1) * B)
                nc.vector.tensor_tensor(bufI[:, half, :], bufI[:, half, :], bufG[:, half, :], ALU.mult)\
                    .then_inc(weighted_ready, 1)
            for k in range(K):
                dve.wait_ge(weighted_ready, k + 1)
                for j in rows(k):
                    ins = nc.vector.tensor_tensor_scan(bufI[:, j, :], bufI[:, j, :], zeros[:, :], 0.0, ALU.add, ALU.add)
            then_wait(ins)

            def add_hidden(a, z):
                x = by_b(X[:, :, a * B:z * B])
                ins = nc.vector.tensor_tensor(x, x, bufI[:, :, a:z].rearrange("p (k b) t -> p k b t", k=K), ALU.add)
                ins.then_inc(hidden_ready, z - a)

            for a, z in ((0, CH), (CH, TS)):
                add_hidden(a, z)
                if a == 0:
                    x, (hi, lo) = X[:, :, 0:CC], (x_parts[:, 0, h] for h in range(2))
                    dve.wait_ge(hidden_ready, CH)
                    nc.vector.tensor_scalar(hi, x, 2.0, None, ALU.mult).then_inc(x2_hi, CH)
                    dve.wait_ge(x2_hi, CH)
                    nc.vector.scalar_tensor_tensor(lo, x, 2.0, hi, ALU.mult, ALU.subtract).then_inc(x2_parts, CH)
                    for slot in (1, 2):
                        nc.vector.tensor_scalar(cell_add[:, :, slot], flat(cond[:, :, :]), 1.0, None, ALU.mult)
                    nc.vector.tensor_scalar(halves(hh_), cond[:, :, :], 2.0, None, ALU.mult).then_inc(s_hi_ready, 1)
                    dve.wait_ge(s_hi_ready, 1)
                    nc.vector.scalar_tensor_tensor(halves(hl_), cond[:, :, :], 2.0, halves(hh_),
                                                   ALU.mult, ALU.subtract).then_inc(s_lo_ready, 1)
            dve.wait_ge(sgc_ready, 1)
            nc.vector.tensor_tensor(silu[:, :, :], sgc[:, :, :], cond[:, :, :], ALU.mult).then_inc(silu_ready, 1)

            def x3_high(t0, a, z, parity):
                n = (z - a) * B
                nc.vector.tensor_tensor(x3_parts[:, parity, 0, :, a * B:z * B], X[:, :, bass.ds((t0 + a) * B, n)],
                                        zeros[:, 0:K * n].rearrange("p (k n) -> p k n", k=K), ALU.add)\
                    .then_inc(x3_hi, z - a)

            def x3_low(t0, a, z, parity):
                hi, lo = (x3_parts[:, parity, h, :, a * B:z * B] for h in range(2))
                nc.vector.tensor_tensor(lo, X[:, :, bass.ds((t0 + a) * B, (z - a) * B)], hi, ALU.subtract)\
                    .then_inc(x3_split, z - a)

            nothing = lambda: None

            def step2(t, s, between, t0, parity):
                c, u = divmod(s, CH)

                def shares(gates, psum):
                    return nc.vector.tensor_reduce(gates[:, :, :], psum[c % 2][:, u].rearrange("p g h b -> p g b h"),
                                                   AX_X, ALU.add)

                dve.wait_ge(gf_psum, t + 1)
                shares(gf_sum, GF).then_inc(gf_ready, 1)
                between()
                dve.wait_ge(o_psum, t + 1)
                shares(o_sum, O).then_inc(o_ready, 1)
                dve.wait_ge(gf_tanh, t + 1)
                nc.vector.tensor_tensor_scan(flat3(cells[:, :, :]), flat3(cell_mul), flat3(cell_add), 0.0,
                                             ALU.mult, ALU.add).then_inc(c_ready, 1)
                dve.wait_ge(c_ready, t + 1)
                nc.vector.tensor_copy(cell_add[:, :, 1:3], cells[:, :, 4:5].broadcast_to([P, K * B, 2]))
                if s == CH + 1:
                    x3_high(t0, 0, CH, parity)
                if s == CH + 2:
                    x3_low(t0, 0, CH, parity)
                if s == TS - 1:
                    x3_high(t0, CH, TS - 1, parity)
                dve.wait_ge(c_tanh, t + 1)
                nc.vector.scalar_tensor_tensor(hh_, gz[:, :], 1.0, tcell[:, :], ALU.add, ALU.mult)\
                    .then_inc(s_hi_ready, 1)
                h = h32[:, s % 2, :]
                nc.vector.scalar_tensor_tensor(h, gz[:, :], 1.0, tcell[:, :], ALU.add, ALU.mult)\
                    .then_inc(s_32_ready, 1)
                dve.wait_ge(s_32_ready, t + 1)
                nc.vector.tensor_tensor(hl_, h, hh_, ALU.subtract).then_inc(s_lo_ready, 1)
                xs = X[:, :, bass.ds(t * B, B)]
                nc.vector.scalar_tensor_tensor(xs, halves(h), 0.5, xs, ALU.mult, ALU.add).then_inc(x3_added, 1)
                if s == TS - 1:
                    dve.wait_ge(x3_added, t + 1)
                    x3_high(t0, TS - 1, TS, parity)
                    dve.wait_ge(x3_hi, t + 1)
                    x3_low(t0, CH, TS, parity)

            def split_high(t, s, nets):
                n = len(blocks_of(s, nets))
                if n:
                    dve.wait_ge(gelu_ready, t + 1)
                    dve.wait_ge(down_done, t - 1 if s == 1 else t)
                    nc.vector.tensor_copy(Gh[:, s % 2, 0:n, :], G[:, s % 2, 0:n, :])\
                        .then_inc(gh_ready, 2 if s == LAST_UP else 1)

            def split_low(t, s, nets):
                n = len(blocks_of(s - 1, nets))
                if n:
                    dve.wait_ge(gh_ready, t)
                    nc.vector.tensor_tensor(Gl[:, (s - 1) % 2, 0:n, :], G[:, (s - 1) % 2, 0:n, :],
                                            Gh[:, (s - 1) % 2, 0:n, :], ALU.subtract)\
                        .then_inc(gl_ready, 2 if s - 1 == LAST_UP else 1)

            def finished_rows(t, s, nets, t0):
                for p, m, f in blocks_of(s - 1, nets):
                    if f == FC - 1:
                        dve.wait_ge(down_done, t + 1)
                        src, bias = bank[5 + p % 2][:, 0:D], eb2b[:, m, :]
                        if m == 0:
                            dst, src, bias = X[:, :, bass.ds(t0 * B, TC)], halves(src), halves(bias)
                        else:
                            dst = routed_rows(t0, m)
                        nc.vector.scalar_tensor_tensor(dst, src, UNSCALE, bias, ALU.mult, ALU.add).then_inc(y_ready, 1)

            stretches = list(zip(CUTS, CUTS[1:]))

            def stretch_sums(t0, some=range(len(stretches))):
                x = X[:, :, bass.ds(t0 * B, TC)].rearrange("p k (t b) -> p k b t", b=B)
                sums = flat3(part[:, bass.ds(t0, TS), :])
                for i in some:
                    a, z = stretches[i]
                    nc.vector.tensor_reduce(halves(sums[:, i * K * B:(i + 1) * K * B]), x[:, :, :, a:z], AX_X, ALU.add)\
                        .then_inc(part_ready, 1)

            for s in range(TS):
                step2(s, s, nothing, 0, 0)
                if s < N_TILES - 1:
                    add_hidden((s + 1) * TS, (s + 2) * TS)
            dve.wait_ge(in_late, IN_LATE)

            def tile(t0, nets, parity):
                for s in range(TS):
                    t = t0 + s
                    step2(t, s, lambda: split_low(t, s, nets), t0, parity)
                    split_high(t, s, nets)
                    if s < len(stretches):
                        stretch_sums(t0 - TS, (s,))
                    finished_rows(t, s, nets, t0 - TS)

            over_tiles(dve, tile)

            nets = networks(N_TILES - 1)

            def tail_blocks(s):
                split_high(T + s, s, nets)
                split_low(T + s + 1, s + 1, nets)
                finished_rows(T + s, s, nets, T - TS)

            dve.wait_ge(x3_added, T)
            stretch_sums(T - TS)
            dve.wait_ge(part_ready, 3 * N_TILES)
            sums = part[:, :, :].rearrange("p (i t) c -> p i (t c)", t=TS)
            ends = (0, L_HEAD, 2 * L_HEAD, T)
            for g in range(3):
                for i, (a, z) in enumerate(stretches):
                    tiles = [j for j in range(N_TILES) if ends[g] <= j * TS + a and j * TS + z <= ends[g + 1]]
                    ins = nc.vector.tensor_reduce(part9[:, g, i, :],
                                                  sums[:, tiles[0]:tiles[-1] + 1, i * K * B:(i + 1) * K * B]
                                                  .rearrange("p i c -> p c i"), AX_X, ALU.add)
            then_wait(ins)
            then_wait(nc.vector.tensor_reduce(seg[:, :, :], part9[:, :, :, :].rearrange("p g i c -> p g c i"),
                                              AX_X, ALU.add))
            nc.vector.tensor_tensor(agg[:, 1, :], seg[:, 0, :], seg[:, 2, :], ALU.add)
            then_wait(nc.vector.tensor_tensor(agg[:, 2, :], seg[:, 1, :], seg[:, 2, :], ALU.add))
            then_wait(nc.vector.tensor_tensor(agg[:, 0, :], agg[:, 1, :], seg[:, 1, :], ALU.add))
            nc.vector.tensor_scalar(agg[:, 0, :], agg[:, 0, :], 1.0 / T, None, ALU.mult)
            nc.vector.tensor_scalar(agg[:, 1:3, :], agg[:, 1:3, :], 1.0 / (L_HEAD + L_PROPRIO), None, ALU.mult)\
                .then_inc(agg_ready, 1)
            tail_blocks(0)
            dve.wait_ge(gate_psum, 1)
            then_wait(nc.vector.tensor_tensor(mod[:, :], bank[2][0:B, 0:2 * E], sbb[:, E:3 * E], ALU.add))
            then_wait(nc.vector.tensor_tensor(lg[:, :], bank[3][0:B, 0:E], sbb[:, 0:E], ALU.add))
            then_wait(nc.vector.scalar_tensor_tensor(lg[:, :], mod[:, 0:E], 1.0, lg[:, :], ALU.add, ALU.mult))
            then_wait(nc.vector.tensor_tensor(lg[:, :], lg[:, :], mod[:, E:2 * E], ALU.add))
            then_wait(nc.vector.reduce_max(mx[:, :], lg[:, :], AX_X))
            nc.vector.tensor_scalar(mx[:, :], mx[:, :], -1.0, None, ALU.mult).then_inc(mx_ready, 1)

            tail_blocks(1)
            dve.wait_ge(ex_ready, 1)
            then_wait(nc.vector.reduce_sum(sm[:, :], ex[:, :], AX_X))
            then_wait(nc.vector.reciprocal(rs[:, :], sm[:, :]))
            then_wait(nc.vector.tensor_scalar(sc[:, :], ex[:, :], rs[:, 0:1], None, ALU.mult))
            scj = sc[:, None, :].broadcast_to([B, E, E])
            sce = sc[:, :, None].broadcast_to([B, E, E])
            then_wait(nc.vector.tensor_tensor(g3[:, :, :], scj, sce, ALU.is_gt))
            then_wait(nc.vector.tensor_tensor(q3[:, :, :], scj, sce, ALU.is_equal))
            then_wait(nc.vector.tensor_tensor(q3[:, :, :], q3[:, :, :], low[:, :].rearrange("p (e j) -> p e j", e=E), ALU.mult))
            then_wait(nc.vector.tensor_tensor(g3[:, :, :], g3[:, :, :], q3[:, :, :], ALU.add))
            then_wait(nc.vector.reduce_sum(rank[:, :], g3[:, :, :], AX_X))
            then_wait(nc.vector.scalar_tensor_tensor(sel5[:, 0:E], rank[:, :], 1.5, sc[:, :], ALU.is_lt, ALU.mult))
            then_wait(nc.vector.reduce_sum(sm[:, :], sel5[:, 0:E], AX_X))
            then_wait(nc.vector.tensor_scalar(sm[:, :], sm[:, :], EPS, None, ALU.add))
            then_wait(nc.vector.reciprocal(rs[:, :], sm[:, :]))
            then_wait(nc.vector.tensor_scalar(sel5[:, 0:E], sel5[:, 0:E], rs[:, 0:1], None, ALU.mult))
            nc.vector.memset(sel5[:, E:E + 1], 1.0).then_inc(sel_ready, 1)

            def add_routed(tiles):
                written = {}
                for place in range(E):
                    for i in tiles:
                        nets = networks(i)[1:]
                        n = place - (E - len(nets))
                        if n >= 0:
                            m = nets[n]
                            row, y = X[:, :, i * TC:(i + 1) * TC], halves(routed_rows(i * TS, m))
                            if n:
                                dve.wait_ge(dve_step, written[i])
                            ins = nc.vector.scalar_tensor_tensor(row if m < E else y, y, wtok[:, i, m - 1:m], row,
                                                                 ALU.mult, ALU.add)
                            if m < E:
                                steps[0] += 1
                                ins.then_inc(dve_step, 1)
                                written[i] = steps[0]
                            else:
                                ins.then_inc(out_ready, 1)

            n_rows = [len(networks(i)) for i in range(N_TILES)]
            rows_by_dve = [i for i in range(N_TILES - 1) if i not in BY_POOL]
            for s in range(2, TS):
                tail_blocks(s)
                if s == ROUTED:
                    dve.wait_ge(wsel_psum, 1)
                    nc.vector.tensor_tensor(wtok[:, :, :], bank[4][:, None, 0:E].broadcast_to([P, N_TILES, E]),
                                            mtok[:, :, :], ALU.mult).then_inc(wtok_ready, 1)
                    dve.wait_ge(wtok_ready, 1)
                    dve.wait_ge(y_ready, sum(n_rows[:-1]))
                if s > ROUTED:
                    slots = TS - ROUTED - 1
                    k = s - ROUTED - 1
                    if k % 2:
                        pair = (k // 2, slots // 2)
                        add_routed(rows_by_dve[pair[0] * len(rows_by_dve) // pair[1]:
                                               (pair[0] + 1) * len(rows_by_dve) // pair[1]])
            dve.wait_ge(y_ready, sum(n_rows))
            add_routed([N_TILES - 1])


def kernel(**inputs):
    import numpy as np
    import concourse.bacc as bacc
    from concourse.bass_utils import run_bass_kernel_spmd as run

    g = {n: np.asarray(a) for n, a in inputs.items()}

    def halves_first(w):
        return w.reshape(K, P, -1).transpose(1, 0, 2)

    def columns(*bs):
        return np.concatenate(bs).reshape(-1, P).T

    def gates(*ws):
        return np.stack([halves_first(w) for w in ws], axis=1).reshape(P, -1)

    c = lambda n: g["L0_cond_" + n]
    f = lambda n: g["L1_cond_" + n]
    m = lambda n: g["L3_cond_" + n]
    t = np.arange(T)
    mask = np.ones((E, T), np.float32)
    mask[1, L_HEAD:2 * L_HEAD] = 0.0
    mask[2, :L_HEAD] = 0.0
    by_row = mask.reshape(E, N_TILES, TS, 1).repeat(B, axis=3).reshape(E, N_TILES, P)
    arrays = {
        "xT": g["x"].transpose(2, 1, 0).reshape(K, P, TOK).transpose(1, 0, 2),
        "condT": halves_first(g["cond_1024"].T),
        "w0": gates(c("W_r"), c("W_z"), c("W")),
        "u0": gates(c("U_r"), c("U_z"), c("U")),
        "c0": gates(c("C_r"), c("C_z"), c("C")).reshape(P, 3, K, D),
        "b0": columns(c("b_r"), c("b_z"), c("b")),
        "w1": gates(f("W_f").T, f("W_i").T, f("W_h").T),
        "b1": columns(f("b_f"), f("b_i"), f("b_h")),
        "wk": gates(*(g["L2_cond_Wk"][:, i * D:(i + 1) * D] for i in (2, 0, 1))),
        "wr": gates(*(g["L2_cond_Wr"][:, i * D:(i + 1) * D] for i in (2, 0, 1))),
        "gate_w": m("gate_w").reshape(3 * K, P, E).transpose(1, 0, 2),
        "time_w": halves_first(m("time_w")),
        "small_b": np.broadcast_to(np.concatenate([m("gate_b"), m("time_b")]), (B, 3 * E)),
        "eb1": columns(m("sb1"), m("eb1").ravel()),
        "eb2": np.broadcast_to(np.concatenate([m("sb2")[None], m("eb2")]), (P, E + 1, D)),
        "ew1": np.concatenate([m("sw1")[None], m("ew1")]).reshape(E + 1, K, P, HID).transpose(2, 0, 1, 3).reshape(P, -1),
        "ew2": np.concatenate([m("sw2")[None], m("ew2")]).reshape(E + 1, FC, P, D).transpose(2, 0, 1, 3).reshape(P, -1),
        "ident": np.eye(P, dtype=np.float32),
        "bsel": (np.arange(P)[None] % B == np.arange(B)[:, None]).astype(np.float32),
        "lower": np.broadcast_to(np.tril(np.ones((E, E), np.float32), -1).reshape(1, E * E), (B, E * E)),
        "mask_tok": by_row.transpose(2, 1, 0),
    }
    nc = bacc.Bacc("TRN2", target_bir_lowering=False, num_devices=1)
    arrays = {n: np.ascontiguousarray(a) for n, a in arrays.items()}
    aps = {n: nc.dram_tensor("in_" + n, a.shape, mybir.dt.from_np(a.dtype), kind="ExternalInput").ap()
           for n, a in arrays.items()}
    out = nc.dram_tensor("out_0", (B, T, D), F32, kind="ExternalOutput").ap()
    build(nc, **aps, out=out)
    r = run(nc, [{"in_" + n: a for n, a in arrays.items()}], core_ids=[0])
    return r.results[0]["out_0"]
```
